# Optimizing a Trainium2 kernel written in Bass

```python
import numpy as np
import jax
import jax.numpy as jnp

def _softmax(x, axis=-1):
    return jax.nn.softmax(x, axis=axis)

def _gelu(x):
    return jax.nn.gelu(x, approximate=True)

def _silu(x):
    return jax.nn.silu(x)

def _sigmoid(x):
    return jax.nn.sigmoid(x)

def _layernorm(x, axis=-1, eps=1e-05):
    m = jnp.mean(x, axis=axis, keepdims=True)
    v = jnp.var(x, axis=axis, keepdims=True)
    return (x - m) / jnp.sqrt(v + eps)

def _scatter_add(tgt, idx, src, axis=0):
    return tgt.at[idx].add(src)

def _segment_sum(src, seg, n):
    return jax.ops.segment_sum(src, seg, n)
kernel_name = 'mk_seq_preln_d1_jaxref_r2_bf8abe'

def setup_inputs(seed: int=0):
    np.random.seed(seed)
    _w = jnp.asarray

    def _L0_attn_setup():
        import jax, jax.numpy as jnp
        import numpy as np
        import math
        B, T, E, H = (4, 1024, 512, 16)
        D = E // H
        rng = jax.random.key(seed)
        k1, k2, k3, k4, k5 = jax.random.split(rng, 5)
        scale_w = 1.0 / math.sqrt(E)
        return {'query': jax.random.normal(k1, (B, T, E), jnp.float32), 'key': jax.random.normal(k2, (B, T, E), jnp.float32), 'value': jax.random.normal(k3, (B, T, E), jnp.float32), 'in_proj_weight': jax.random.normal(k4, (3 * E, E), jnp.float32) * scale_w, 'out_proj_weight': jax.random.normal(k5, (E, E), jnp.float32) * scale_w}
    _L0_attn_in = _L0_attn_setup()

    def _L0_ffn_setup():
        import jax, jax.numpy as jnp
        import numpy as np
        from jax import lax
        T, B, I, M, O = (128, 64, 512, 512, 512)

        def _xavier(key, shape):
            fan_out, fan_in = shape
            limit = float(np.sqrt(6.0 / (fan_in + fan_out)))
            return jax.random.uniform(key, shape, jnp.float32, -limit, limit)
        key = jax.random.key(seed)
        ks = jax.random.split(key, 9)
        x = jax.random.normal(ks[0], (T, B, I), jnp.float32)
        return {'x': x, 'wf': _xavier(ks[1], (M, I)), 'uf': _xavier(ks[2], (M, M)), 'bf': jnp.zeros((M,), jnp.float32), 'wi': _xavier(ks[3], (M, I)), 'ui': _xavier(ks[4], (M, M)), 'bi': jnp.zeros((M,), jnp.float32), 'wc': _xavier(ks[5], (M, I)), 'uc': _xavier(ks[6], (M, M)), 'bc': jnp.zeros((M,), jnp.float32), 'wo': _xavier(ks[7], (O, I)), 'uo': _xavier(ks[8], (O, M)), 'bo': jnp.zeros((O,), jnp.float32), 'in_c': jnp.zeros((M,), jnp.float32)}
    _L0_ffn_in = _L0_ffn_setup()
    _d = {'L0_attn_query': _L0_attn_in['query'], 'L0_attn_key': _L0_attn_in['key'], 'L0_attn_value': _L0_attn_in['value'], 'L0_attn_in_proj_weight': _L0_attn_in['in_proj_weight'], 'L0_attn_out_proj_weight': _L0_attn_in['out_proj_weight'], 'L0_ffn_wf': _L0_ffn_in['wf'], 'L0_ffn_uf': _L0_ffn_in['uf'], 'L0_ffn_bf': _L0_ffn_in['bf'], 'L0_ffn_wi': _L0_ffn_in['wi'], 'L0_ffn_ui': _L0_ffn_in['ui'], 'L0_ffn_bi': _L0_ffn_in['bi'], 'L0_ffn_wc': _L0_ffn_in['wc'], 'L0_ffn_uc': _L0_ffn_in['uc'], 'L0_ffn_bc': _L0_ffn_in['bc'], 'L0_ffn_wo': _L0_ffn_in['wo'], 'L0_ffn_uo': _L0_ffn_in['uo'], 'L0_ffn_bo': _L0_ffn_in['bo'], 'L0_ffn_in_c': _L0_ffn_in['in_c']}
    _x0 = _d['L0_attn_query']
    _d['L0_attn_query'] = jax.random.normal(jax.random.fold_in(jax.random.key(seed), 1), (8, 1024, 512), dtype=_x0.dtype)
    del _x0
    return _d

def reference(L0_attn_query, L0_attn_key, L0_attn_value, L0_attn_in_proj_weight, L0_attn_out_proj_weight, L0_ffn_wf, L0_ffn_uf, L0_ffn_bf, L0_ffn_wi, L0_ffn_ui, L0_ffn_bi, L0_ffn_wc, L0_ffn_uc, L0_ffn_bc, L0_ffn_wo, L0_ffn_uo, L0_ffn_bo, L0_ffn_in_c):

    def _L0_attn_ref(query, key, value, in_proj_weight, out_proj_weight):
        import jax, jax.numpy as jnp
        import numpy as np
        import math
        B, T, E, H = (4, 1024, 512, 16)
        D = E // H
        b, t, e = query.shape
        qkv = jnp.einsum('bte,fe->btf', query, in_proj_weight).reshape(b, t, 3, H, D)
        q = jnp.transpose(qkv[:, :, 0], (0, 2, 1, 3))
        k = jnp.transpose(qkv[:, :, 1], (0, 2, 1, 3))
        v = jnp.transpose(qkv[:, :, 2], (0, 2, 1, 3))
        q = q / math.sqrt(D)
        scores = jnp.einsum('bhqd,bhkd->bhqk', q, k)
        pos = jnp.arange(t)
        causal = pos[:, None] >= pos[None, :]
        scores = jnp.where(causal[None, None], scores, jnp.float32(-jnp.inf))
        attn = jax.nn.softmax(scores, axis=-1)
        out = jnp.einsum('bhqk,bhkd->bhqd', attn, v)
        out = jnp.transpose(out, (0, 2, 1, 3)).reshape(b, t, e)
        out = jnp.einsum('bte,fe->btf', out, out_proj_weight)
        return out

    def _L0_ffn_ref(x, wf, uf, bf, wi, ui, bi, wc, uc, bc, wo, uo, bo, in_c):
        import jax, jax.numpy as jnp
        import numpy as np
        from jax import lax
        T, B, I, M, O = (128, 64, 512, 512, 512)

        def _xavier(key, shape):
            fan_out, fan_in = shape
            limit = float(np.sqrt(6.0 / (fan_in + fan_out)))
            return jax.random.uniform(key, shape, jnp.float32, -limit, limit)
        batch = x.shape[1]
        c0 = jnp.broadcast_to(in_c, (batch, in_c.shape[0]))

        def step(c, xt):
            ft = jax.nn.sigmoid(xt @ wf.T + c @ uf.T + bf)
            it = jax.nn.sigmoid(xt @ wi.T + c @ ui.T + bi)
            gt = jnp.tanh(xt @ wc.T + c @ uc.T + bc)
            c = ft * c + it * gt
            return (c, None)
        c_final, _ = lax.scan(step, c0, x)
        h = jnp.tanh(jnp.einsum('tbi,oi->tbo', x, wo) + c_final @ uo.T + bo)
        return h
    x = L0_attn_query
    x = x + _L0_attn_ref(_layernorm(x, axis=-1), L0_attn_key, L0_attn_value, L0_attn_in_proj_weight, L0_attn_out_proj_weight)
    x = x + _L0_ffn_ref(_layernorm(x, axis=-1), L0_ffn_wf, L0_ffn_uf, L0_ffn_bf, L0_ffn_wi, L0_ffn_ui, L0_ffn_bi, L0_ffn_wc, L0_ffn_uc, L0_ffn_bc, L0_ffn_wo, L0_ffn_uo, L0_ffn_bo, L0_ffn_in_c)
    return x

_drawn_inputs = setup_inputs


def setup_inputs(seed=0):
    import zlib

    import numpy as np

    out = dict(_drawn_inputs(seed))
    spreads = {'L0_ffn_bf': (0.0, 0.795),
     'L0_ffn_bi': (0.0, 0.713),
     'L0_ffn_bc': (0.0, 0.1),
     'L0_ffn_bo': (0.0, 0.1),
     'L0_ffn_in_c': (0.0, 0.8)}
    factors = {}
    for name, (base, spread) in spreads.items():
        noise = np.random.default_rng([zlib.crc32(name.encode()), seed]).standard_normal(out[name].shape)
        drawn = base * np.exp(spread * noise) if base else spread * noise
        out[name] = jnp.asarray(drawn.astype(out[name].dtype))
    for name, factor in factors.items():
        out[name] = (out[name] * factor).astype(out[name].dtype)
    return out
```

```python
from contextlib import ExitStack

import concourse.bass as bass
from concourse import mybir

ALU = mybir.AluOpType
ACT = mybir.ActivationFunctionType
AX_X = mybir.AxisListType.X
F32 = mybir.dt.float32
F16 = mybir.dt.float16
BF16 = mybir.dt.bfloat16
U32 = mybir.dt.uint32
POOL_MAX = bass.bass_isa.ReduceOp.max

P = 128
B, T, E = 8, 1024, 512
H, D = 16, 32
TT = T // P
EC = E // P
HG = P // D
NG = H // HG
HALF = T // 2
LN_EPS = 1e-5
HL = 2
EXPONENT = 0x7F800000
W_TOP = 4.0
SHIFT_ROW = 32768.0
MASKED = -3.0e38
PASSES = ((0, 0), (0, 1), (1, 0))


class Chain:

    def __init__(self, eng, sem, base=0):
        self.eng, self.sem, self.base, self.count = eng, sem, base, 0

    def after(self, instruction):
        instruction.then_inc(self.sem, 1)
        self.count += 1
        self.eng.wait_ge(self.sem, self.base + self.count)


def prepare_weights(nc, tag, jobs, inv, ident16, global_rows, scratch_v=None, c_scale=None):
    J = len(jobs)
    M = max(len(j) for j in jobs)
    with ExitStack() as ctx:
        def sb(name, shape, dt):
            return ctx.enter_context(nc.sbuf_tensor(f"{tag}_{name}", shape, dt))

        def sem(name):
            return ctx.enter_context(nc.semaphore(f"{tag}_{name}"))

        nat = sb("nat", [P, 2, M * EC, E], F32)
        part = sb("part", [P, 2, HL, M * EC, E], F16)
        rowmax = sb("rowmax", [P, M * EC], F32)
        pairmax = sb("pairmax", [P, EC], F32)
        onemax = sb("onemax", [P, 1], F32)
        allmax = sb("allmax", [P, 1], F32)
        scale = sb("scale", [P, EC], F32)
        vrow = sb("vrow", [P, E], F32)
        tp = ctx.enter_context(nc.psum_tensor(f"{tag}_tp", [P, 4, HL * EC * P], F16))
        loaded, nat_used = [sem("loaded0"), sem("loaded1")], sem("nat_used")
        transposed, evacuated, own = sem("transposed"), sem("evacuated"), sem("own")
        max_in, max_out = sem("max_in"), sem("max_out")
        vinv_ready, vinv_stored, vinv_loaded = sem("vinv_ready"), sem("vinv_stored"), sem("vinv_loaded")
        block = ctx.enter_context(nc.Block())

        loads_until = [16 * sum(len(other) for other in jobs[j % 2:j + 1:2]) for j in range(J)]
        tiles_until = [0]
        for job in jobs:
            tiles_until.append(tiles_until[-1] + len(job) * EC)

        @block.sync
        def _(sp):
            for j, job in enumerate(jobs):
                if j >= 2:
                    sp.wait_ge(nat_used, j - 1)
                for m, (w, _, _) in enumerate(job):
                    sp.dma_start(nat[:, j % 2, m * EC:(m + 1) * EC, :],
                                 w.rearrange("(t p) e -> p t e", p=P)).then_inc(loaded[j % 2], 16)
            if scratch_v is not None:
                v_job, row = scratch_v
                sp.wait_ge(vinv_ready, 1)
                sp.dma_start(row.rearrange("(t p) -> p t", p=P), inv[:, v_job, :]).then_inc(vinv_stored, 16)
                sp.wait_ge(vinv_stored, 16)
                sp.dma_start(vrow[:, :], row.partition_broadcast(P)).then_inc(vinv_loaded, 16)

        @block.gpsimd
        def _(pool):
            for k in range(len(global_rows)):
                pool.wait_ge(max_in, k + 1)
                nc.gpsimd.partition_all_reduce(allmax[:, :], onemax[:, :], P, POOL_MAX).then_inc(max_out, 1)

        @block.vector
        def _(dve):
            ch = Chain(dve, own)
            n_global = 0
            for j, job in enumerate(jobs):
                m = len(job)
                w = nat[:, j % 2]
                dve.wait_ge(loaded[j % 2], loads_until[j])
                if scratch_v is not None and j == J - 1:
                    dve.wait_ge(vinv_loaded, 16)
                    ch.after(nc.vector.tensor_tensor(w[:, 0:EC, :], w[:, 0:EC, :],
                                                     vrow[:, :].unsqueeze(1).broadcast_to([P, EC, E]), ALU.mult))
                if c_scale is not None and m == 2:
                    ch.after(nc.vector.tensor_scalar(w[:, EC:2 * EC, :], w[:, EC:2 * EC, :],
                                                     c_scale[:, 0:1], None, ALU.mult))
                ch.after(nc.vector.tensor_reduce(rowmax[:, 0:m * EC], w[:, 0:m * EC, :], AX_X, ALU.max,
                                                 apply_absolute_value=True))
                top = rowmax[:, 0:EC]
                if m == 2:
                    ch.after(nc.vector.tensor_tensor(pairmax[:, :], rowmax[:, 0:EC], rowmax[:, EC:2 * EC], ALU.max))
                    top = pairmax[:, :]
                if j in global_rows:
                    ch.after(nc.vector.tensor_reduce(onemax[:, :], top, AX_X, ALU.max))
                    n_global += 1
                    nc.vector.engine_nop().then_inc(max_in, 1)
                    dve.wait_ge(max_out, n_global)
                    top = allmax[:, 0:1].broadcast_to([P, EC])
                ch.after(nc.vector.tensor_scalar(scale[:, :], top, 1e-15, None, ALU.max))
                ch.after(nc.vector.tensor_scalar(scale[:, :].bitcast(U32), scale[:, :].bitcast(U32),
                                                 EXPONENT, None, ALU.bitwise_and))
                ch.after(nc.vector.tensor_scalar(inv[:, j, :], scale[:, :], 1.0 / W_TOP, None, ALU.mult))
                if scratch_v is not None and j == scratch_v[0]:
                    nc.vector.engine_nop().then_inc(vinv_ready, 1)
                ch.after(nc.vector.reciprocal(scale[:, :], inv[:, j, :]))
                if j >= 2:
                    dve.wait_ge(transposed, tiles_until[j - 1])
                for k in range(m):
                    ws = w[:, k * EC:(k + 1) * EC, :]
                    ch.after(nc.vector.tensor_tensor(ws, ws, scale[:, :].unsqueeze(2).broadcast_to([P, EC, E]),
                                                     ALU.mult))
                    hi = part[:, j % 2, 0, k * EC:(k + 1) * EC, :]
                    lo = part[:, j % 2, 1, k * EC:(k + 1) * EC, :]
                    ch.after(nc.vector.tensor_copy(hi, ws))
                    last = nc.vector.tensor_tensor(lo, ws, hi, ALU.subtract)
                    if k == m - 1:
                        last.then_inc(nat_used, 1)
                    else:
                        ch.after(last)

        @block.tensor
        def _(pe):
            n = 0
            for j, job in enumerate(jobs):
                pe.wait_ge(nat_used, j + 1)
                for k in range(len(job) * EC):
                    if n >= 4:
                        pe.wait_ge(evacuated, n - 3)
                    for hl in range(HL):
                        for e in range(EC):
                            last = nc.tensor.transpose(tp[:, n % 4, (hl * EC + e) * P:(hl * EC + e + 1) * P],
                                                       part[:, j % 2, hl, k, e * P:(e + 1) * P], ident16[:, :])
                    last.then_inc(transposed, 1)
                    n += 1

        @block.scalar
        def _(act):
            n = 0
            for job in jobs:
                for _, target, col in job:
                    for t in range(EC):
                        act.wait_ge(transposed, n + 1)
                        nc.scalar.activation(
                            target[:, :, :, col + t * P:col + (t + 1) * P],
                            tp[:, n % 4, :].rearrange("p (l e f) -> p l e f", l=HL, e=EC),
                            ACT.Copy).then_inc(evacuated, 1)
                        n += 1


def normalise_tokens(nc, tag, src, dst_t, ident16, outproj=None):
    with ExitStack() as ctx:
        def sb(name, shape, dt):
            return ctx.enter_context(nc.sbuf_tensor(f"{tag}_{name}", shape, dt))

        def sem(name):
            return ctx.enter_context(nc.semaphore(f"{tag}_{name}"))

        def slots(name):
            return [sem(f"{name}{s}") for s in range(2)]

        x = sb("x", [P, 2, TT, E], F32)
        xh = sb("xh", [P, 2, E], F32)
        hi = sb("hi", [P, 2, E], F16)
        lo = sb("lo", [P, 2, E], F16)
        stats = sb("stats", [P, TT, 6], F32)
        mean2, diff, dev = (sb(name, [P, TT], F32) for name in ("mean2", "diff", "dev"))
        diff2, dev_all = (sb(name, [P, TT], F32) for name in ("diff2", "dev_all"))
        var = sb("var", [P, TT], F32)
        std = sb("std", [P, TT], F32)
        rstd = sb("rstd", [P, TT], F32)
        shift = sb("shift", [P, TT], F32)
        xt = sb("xt", [P, 2, HL, EC, T], F16)
        tp = ctx.enter_context(nc.psum_tensor(f"{tag}_tp", [P, 4, HL * EC * P], F16))
        loaded, lo_ready, xh_ready = slots("loaded"), sem("lo_ready"), sem("xh_ready")
        stats_ready, moment, var_ready = sem("stats_ready"), sem("moment"), sem("var_ready")
        std_ready, inverse_ready, rstd_ready = sem("std_ready"), sem("inverse_ready"), sem("rstd_ready")
        hi_ready, transposed, evacuated, stored = sem("hi_ready"), sem("transposed"), sem("evacuated"), slots("stored")
        if outproj:
            o_parts, w_out, inv_out, x1 = outproj
            ot = sb("ot", [P, 2, HL, NG, T], F16)
            y = sb("y", [P, 2, E], F32)
            inv_row = sb("inv_row", [P, E], F32)
            yp = ctx.enter_context(nc.psum_tensor(f"{tag}_yp", [P, 4, E], F32))
            o_loaded, y_ready, y_read = slots("o_loaded"), sem("y_ready"), sem("y_read")
            x1_ready, x1_stored, row_loaded = sem("x1_ready"), slots("x1_stored"), sem("row_loaded")
        block = ctx.enter_context(nc.Block())
        X_CREDIT, TP_CREDIT, PART_CREDIT, Y_CREDIT, STORE_CREDIT = TT, 4, 2, 4, 16

        @block.sync
        def _(sp):
            for s in range(2):
                sp.sem_inc(stored[s], STORE_CREDIT)
                if outproj:
                    sp.sem_inc(x1_stored[s], STORE_CREDIT)
            if outproj:
                sp.dma_start(inv_row[:, :], inv_out.partition_broadcast(P)).then_inc(row_loaded, 16)

            def load(b, s):
                sp.dma_start(x[:, s], src[bass.ds(b, 1)].rearrange("o (t p) e -> p (o t) e", p=P)
                             ).then_inc(loaded[s], 16)
                if outproj:
                    sp.dma_start(ot[:, s], o_parts[bass.ds(b, 1)].rearrange("o p l g t -> p (o l) g t")
                                 ).then_inc(o_loaded[s], 16)

            def pair(i, last):
                for s in range(2):
                    b = i * 2 + s
                    if not (last and s == 1):
                        sp.wait_ge(lo_ready, i * (2 * TT) + s * TT + TT)
                        if outproj:
                            sp.wait_ge(x1_stored[1 - s], i * 16 + (STORE_CREDIT if s == 0 else 16 + STORE_CREDIT))
                        load(b + 1, 1 - s)
                    if outproj:
                        sp.wait_ge(x1_ready, i * (2 * TT) + (s + 1) * TT)
                        sp.dma_start(x1[bass.ds(b, 1)].rearrange("o (t p) e -> p (o t) e", p=P), x[:, s]
                                     ).then_inc(x1_stored[s], 16)
                    sp.wait_ge(evacuated, i * (2 * TT) + (s + 1) * TT + TP_CREDIT)
                    sp.dma_start(dst_t[bass.ds(b, 1)].rearrange("o p l e t -> p (o l) e t"), xt[:, s]
                                 ).then_inc(stored[s], 16)

            load(0, 0)
            with sp.Fori(0, B // 2 - 1) as i:
                pair(i, False)
            pair(B // 2 - 1, True)
            for s in range(2):
                sp.wait_ge(stored[s], 16 * (B // 2) + STORE_CREDIT)
                if outproj:
                    sp.wait_ge(x1_stored[s], 16 * (B // 2) + STORE_CREDIT)

        @block.vector
        def _(dve):
            dve.sem_inc(lo_ready, X_CREDIT)
            if outproj:
                dve.sem_inc(y_read, Y_CREDIT)
                dve.wait_ge(row_loaded, 16)
            with dve.Fori(0, B // 2) as i:
                for s in range(2):
                    n = i * (2 * TT) + s * TT
                    dve.wait_ge(loaded[s], i * 16 + 16)
                    for t in range(TT):
                        if outproj:
                            dve.wait_ge(y_ready, n + t + 1)
                            nc.vector.tensor_tensor(y[:, t % 2], yp[:, t % 4], inv_row[:, :], ALU.mult
                                                    ).then_inc(y_read, 1)
                            dve.wait_ge(y_read, n + t + 1 + Y_CREDIT)
                            nc.vector.tensor_tensor(x[:, s, t], x[:, s, t], y[:, t % 2], ALU.add
                                                    ).then_inc(x1_ready, 1)
                            dve.wait_ge(x1_ready, n + t + 1)
                        nc.vector.bn_stats(stats[:, t], x[:, s, t]).then_inc(stats_ready, 1)
                    dve.wait_ge(stats_ready, n + TT)
                    step = i * 10 + s * 5
                    nc.vector.tensor_tensor(mean2[:, :], stats[:, :, 1], stats[:, :, 4], ALU.add).then_inc(moment, 1)
                    nc.vector.tensor_tensor(diff[:, :], stats[:, :, 1], stats[:, :, 4], ALU.subtract).then_inc(moment, 1)
                    nc.vector.tensor_tensor(dev[:, :], stats[:, :, 2], stats[:, :, 5], ALU.add).then_inc(moment, 1)
                    dve.wait_ge(moment, step + 3)
                    nc.vector.tensor_tensor(diff2[:, :], diff[:, :], diff[:, :], ALU.mult).then_inc(moment, 1)
                    dve.wait_ge(moment, step + 4)
                    nc.vector.scalar_tensor_tensor(dev_all[:, :], diff2[:, :], E / 4.0, dev[:, :], ALU.mult, ALU.add
                                                   ).then_inc(moment, 1)
                    dve.wait_ge(moment, step + 5)
                    nc.vector.tensor_scalar(var[:, :], dev_all[:, :], 1.0 / E, LN_EPS, ALU.mult, ALU.add
                                            ).then_inc(var_ready, 1)
                    dve.wait_ge(std_ready, i * 2 + s + 1)
                    nc.vector.reciprocal(rstd[:, :], std[:, :]).then_inc(inverse_ready, 1)
                    dve.wait_ge(inverse_ready, i * 2 + s + 1)
                    nc.vector.scalar_tensor_tensor(shift[:, :], mean2[:, :], -0.5, rstd[:, :],
                                                   ALU.mult, ALU.mult).then_inc(rstd_ready, 1)
                    dve.wait_ge(rstd_ready, i * 2 + s + 1)
                    for t in range(TT):
                        nc.vector.tensor_scalar(xh[:, t % 2], x[:, s, t], rstd[:, t:t + 1], shift[:, t:t + 1],
                                                ALU.mult, ALU.add).then_inc(xh_ready, 1)
                        dve.wait_ge(xh_ready, n + t + 1)
                        dve.wait_ge(hi_ready, n + t + 1)
                        nc.vector.tensor_tensor(lo[:, t % 2], xh[:, t % 2], hi[:, t % 2], ALU.subtract
                                                ).then_inc(lo_ready, 1)

        @block.scalar
        def _(act):
            act.sem_inc(evacuated, TP_CREDIT)

            def evacuate(i, s, t):
                k = i * (2 * TT) + s * TT + t
                act.wait_ge(transposed, k + 1 + PART_CREDIT)
                nc.scalar.activation(xt[:, s, :, :, t * P:(t + 1) * P],
                                     tp[:, t % 4, :].rearrange("p (l e f) -> p l e f", l=HL, e=EC),
                                     ACT.Copy).then_inc(evacuated, 1)

            with act.Fori(0, B // 2) as i:
                for s in range(2):
                    n = i * (2 * TT) + s * TT
                    act.wait_ge(var_ready, i * 2 + s + 1)
                    nc.scalar.activation(std[:, :], var[:, :], ACT.Sqrt).then_inc(std_ready, 1)
                    act.wait_ge(stored[s], i * 16 + STORE_CREDIT)
                    act.wait_ge(rstd_ready, i * 2 + s + 1)
                    for t in range(TT):
                        act.wait_ge(transposed, n + t + 1)
                        nc.scalar.activation(hi[:, t % 2], x[:, s, t], ACT.Identity, bias=shift[:, t:t + 1],
                                             scale=rstd[:, t:t + 1]).then_inc(hi_ready, 1)
                        if t >= 1:
                            evacuate(i, s, t - 1)
                    evacuate(i, s, TT - 1)

        @block.tensor
        def _(pe):
            pe.sem_inc(transposed, PART_CREDIT)
            with pe.Fori(0, B // 2) as i:
                for s in range(2):
                    n = i * (2 * TT) + s * TT
                    if outproj:
                        pe.wait_ge(o_loaded[s], i * 16 + 16)
                        for t in range(TT):
                            pe.wait_ge(y_read, n + t + 1)
                            for k, (a, c) in enumerate(PASSES):
                                for g in range(NG):
                                    last = nc.tensor.matmul(
                                        yp[:, t % 4], ot[:, s, a, g, t * P:(t + 1) * P], w_out[:, c, g, :],
                                        start=(k == 0 and g == 0), stop=(k == len(PASSES) - 1 and g == NG - 1))
                            last.then_inc(y_ready, 1)
                    for t in range(TT):
                        pe.wait_ge(lo_ready, n + t + 1 + X_CREDIT)
                        pe.wait_ge(hi_ready, n + t + 1)
                        pe.wait_ge(evacuated, n + t + 1)
                        for l, part in ((0, hi), (1, lo)):
                            for e in range(EC):
                                last = nc.tensor.transpose(tp[:, t % 4, (l * EC + e) * P:(l * EC + e + 1) * P],
                                                           part[:, t % 2, e * P:(e + 1) * P], ident16[:, :])
                        last.then_inc(transposed, 1)


UNITS = HG * EC + HG * TT
CHUNKS = HG * (EC + 2 * EC)
PROJ_TILES = 6
BANK_USES = PROJ_TILES + 1
SCORE_BANKS, PROB_SLOTS, MAX_BANKS, GENS = 3, 4, 2, 4
AHEAD_FROM = 8
MAX_T_AT = 42
COPY_AT = HG * EC + 1
STACK_DMAS = 6 * HG
USES_BEFORE = 2 * PROJ_TILES + 1


def unit_block(u):
    half, r = (0, u) if u < HG * EC else (1, u - HG * EC)
    h, j = divmod(r, EC if half == 0 else TT)
    return half, h, j, max(0, j * P - half * HALF)


def chunk_block(c):
    h, r = divmod(c, CHUNKS // HG)
    if r < EC:
        return h, r, 0, (r + 1) * P, True
    i, second = EC + (r - EC) // 2, (r - EC) % 2
    return (h, i, HALF, (i - EC + 1) * P, True) if second else (h, i, 0, HALF, False)


def attention(nc, xt_dram, o_dram, m_dram, w_qkv, exp_scale, ident16, identb, neg_m, neg_s):
    with ExitStack() as ctx:
        def sb(name, shape, dt):
            return ctx.enter_context(nc.sbuf_tensor(f"at_{name}", shape, dt))

        def ps(name, shape, dt=F32):
            return ctx.enter_context(nc.psum_tensor(f"at_{name}", shape, dt))

        def sem(name):
            return ctx.enter_context(nc.semaphore(f"at_{name}"))

        xt = sb("xt", [P, HL, EC, T], F16)
        stage = sb("stage", [P, 2, HL, T], F16)
        qs = sb("qs", [P, GENS, HG, T], F16)
        ks = sb("ks", [P, GENS, HG, T], F16)
        v = sb("v", [P, GENS, TT, P], F32)
        probs = sb("probs", [P, PROB_SLOTS, HALF], F32)
        ones = sb("ones", [P, D], F32)
        mx = sb("mx", [P, 2, HG, TT], F32)
        mxall = sb("mxall", [P, HG, TT], F32)
        m32 = sb("m32", [P, HG * TT], F32)
        mparts = sb("mparts", [P, P // (HG * TT), HG * TT], F16)
        mt = sb("mt", [2 * HG * TT, P], F16)
        o_raw = sb("o_raw", [P, HALF], F32)
        l_raw = sb("l_raw", [P, HALF], F32)
        l_inv = sb("l_inv", [P, HALF], F32)
        o_norm = sb("o_norm", [P, HALF], F32)
        o_part = sb("o_part", [P, 2, HL, HALF], F16)

        score_ps = ps("score_ps", [P, SCORE_BANKS, HALF])
        max_ps = ps("max_ps", [P, MAX_BANKS, HALF])
        proj_ps = ps("proj_ps", [P, HALF])
        out_ps = ps("out_ps", [P, HALF])
        sum_ps = ps("sum_ps", [P, HALF])

        setup = sem("setup")
        xt_loaded, xt_used = sem("xt_loaded"), sem("xt_used")
        proj_ready, proj_read, hi_done = sem("proj_ready"), sem("proj_read"), sem("hi_done")
        stage_ready, stacked = sem("stage_ready"), sem("stacked")
        chunk_ready, chunk_read, max_stored = sem("chunk_ready"), sem("chunk_read"), sem("max_stored")
        max_step, max_ready, max_t_copied, max_rows = sem("max_step"), sem("max_ready"), sem("max_t_copied"), sem("max_rows")
        scores_ready, exp_done, pv_done = sem("scores_ready"), sem("exp_done"), sem("pv_done")
        sums_ready, out_copied, l_copied = sem("sums_ready"), sem("out_copied"), sem("l_copied")
        norm_step, o_ready, o_stored = sem("norm_step"), sem("o_ready"), [sem("o_stored0"), sem("o_stored1")]
        block = ctx.enter_context(nc.Block())

        def batches(eng, body):
            with eng.Fori(0, B - 1) as b:
                body(b, False)
            body(B - 1, True)

        def ahead(g, by, last):
            return not (last and g + by >= NG)

        @block.sync
        def _(sp):
            def load_tokens(b):
                sp.dma_start(xt[:, :, :, :], xt_dram[bass.ds(b, 1)].rearrange("o p l e t -> p (o l) e t")
                             ).then_inc(xt_loaded, 16)

            def stack_group(gen, uses):
                for which, dst, order in ((0, qs, (0, 1, 0)), (1, ks, (0, 0, 1))):
                    sp.wait_ge(proj_read, uses + 2 * which + 2 + 1)
                    for h in range(HG):
                        for r, l in enumerate(order):
                            sp.dma_start(dst[r * D:(r + 1) * D, gen, h, :], stage[h * D:(h + 1) * D, which, l, :]
                                         ).then_inc(stacked, 16)

            def max_rows_in(gen, uses, group):
                sp.wait_ge(proj_read, uses + 1 + 1)
                if not (isinstance(group, int) and group == 0):
                    sp.wait_ge(max_rows, group * 16)
                sp.dma_start(m_dram.rearrange("r h (i q) -> (r h i) q", q=P), mt[:, :]).then_inc(max_stored, 16)
                sp.wait_ge(max_stored, 16 * (group + 1))
                sp.dma_start(qs[3 * D:3 * D + 2, gen, :, :], m_dram).then_inc(max_rows, 16)

            def store_output(b, g, half):
                sp.wait_ge(o_ready, b * (2 * NG) + 2 * g + half + 1)
                sp.dma_start(o_dram[bass.ds(b, 1), :, :, g, half * HALF:(half + 1) * HALF]
                             .rearrange("o p l t -> p (o l) t"), o_part[:, half, :, :]).then_inc(o_stored[half], 16)

            for half in range(2):
                sp.sem_inc(o_stored[half], 16)
            load_tokens(0)
            stack_group(0, 0)
            stack_group(1, PROJ_TILES)
            max_rows_in(0, 2 * PROJ_TILES, 0)

            def body(b, last):
                for g in range(NG):
                    uses = (b * NG + g) * BANK_USES + USES_BEFORE
                    if ahead(g, 2, last):
                        stack_group((g + 2) % GENS, uses)
                    if g == 1 and not last:
                        sp.wait_ge(proj_ready, uses + PROJ_TILES)
                        load_tokens(b + 1)
                    store_output(b, g, 0)
                    if ahead(g, 1, last):
                        max_rows_in((g + 1) % GENS, uses + (PROJ_TILES if ahead(g, 2, last) else 0), b * NG + g + 1)
                    store_output(b, g, 1)

            batches(sp, body)
            for half in range(2):
                sp.wait_ge(o_stored[half], 16 * B * NG + 16)

        @block.gpsimd
        def _(pool):
            nc.gpsimd.memset(ks[3 * D:P, :, :, :], SHIFT_ROW).then_inc(setup, 1)
            pool.wait_ge(setup, 1)
            nc.gpsimd.memset(ones[:, :], 1.0).then_inc(setup, 1)
            nc.gpsimd.memset(mx[:, :, :, :], MASKED).then_inc(setup, 1)
            nc.gpsimd.memset(mparts[:, :, :], 0.0).then_inc(setup, 1)

        @block.tensor
        def _(pe):
            pe.sem_inc(pv_done, PROB_SLOTS)

            def projection(g, tile, e, uses):
                if e == 0:
                    pe.wait_ge(proj_read, uses + 1)
                for k, (a, c) in enumerate(PASSES):
                    start, stop = k == 0 and e == 0, k == len(PASSES) - 1 and e == EC - 1
                    if tile < 4:
                        which, half = divmod(tile, 2)
                        last = nc.tensor.matmul(proj_ps[:, :],
                                                w_qkv[:, a, e, which * E + g * P:which * E + (g + 1) * P],
                                                xt[:, c, e, half * HALF:(half + 1) * HALF], start=start, stop=stop)
                    else:
                        for i in range(EC):
                            t = (tile - 4) * EC + i
                            last = nc.tensor.matmul(proj_ps[:, i * P:(i + 1) * P], xt[:, a, e, t * P:(t + 1) * P],
                                                    w_qkv[:, c, e, 2 * E + g * P:2 * E + (g + 1) * P],
                                                    start=start and i == 0, stop=stop, skip_group_check=True)
                if e == EC - 1:
                    last.then_inc(proj_ready, 1)

            def max_chunk(gen, c, count):
                h, i, k0, width, diagonal = chunk_block(c)
                pe.wait_ge(chunk_read, count + 1)
                bank = max_ps[:, c % MAX_BANKS]
                last = nc.tensor.matmul(bank[:, 0:width], qs[0:3 * D, gen, h, i * P:(i + 1) * P],
                                        ks[0:3 * D, gen, h, k0:k0 + width], start=True, stop=not diagonal)
                if diagonal:
                    last = nc.tensor.matmul(bank[:, width - P:width], identb[:, :], neg_m[:, :], start=False, stop=True)
                last.then_inc(chunk_ready, 1)

            def max_transpose(uses, count):
                pe.wait_ge(max_ready, count)
                pe.wait_ge(proj_read, uses + 1)
                nc.tensor.transpose(proj_ps[:, :].bitcast(F16)[:, 0:P], mparts[:, :, :].rearrange("p r c -> p (r c)"),
                                    ident16[:, :]).then_inc(proj_ready, 1)

            def scores(gen, u, count):
                _, h, j, q0 = unit_block(u)
                half = unit_block(u)[0]
                diagonal = j * P >= half * HALF
                pe.wait_ge(exp_done, count + 1)
                bank = score_ps[:, u % SCORE_BANKS]
                last = nc.tensor.matmul(bank[:, 0:HALF - q0], ks[0:3 * D + 2, gen, h, j * P:(j + 1) * P],
                                        qs[0:3 * D + 2, gen, h, half * HALF + q0:(half + 1) * HALF],
                                        start=True, stop=not diagonal)
                if diagonal:
                    last = nc.tensor.matmul(bank[:, 0:P], identb[:, :], neg_s[:, :], start=False, stop=True)
                last.then_inc(scores_ready, 1)

            def values(gen, u, count, halves):
                half, h, j, q0 = unit_block(u)
                end = EC - 1 if half == 0 else TT - 1
                pe.wait_ge(exp_done, count + 1 + SCORE_BANKS)
                if h == 0 and j == 0:
                    pe.wait_ge(out_copied, halves + 1)
                    pe.wait_ge(l_copied, halves + 1)
                pt = probs[:, u % PROB_SLOTS, 0:HALF - q0]
                rows = slice(h * D, (h + 1) * D)
                nc.tensor.matmul(out_ps[rows, q0:HALF], v[:, gen, j, rows], pt, start=(j == 0), stop=(j == end),
                                 tile_position=(0, h * D))
                last = nc.tensor.matmul(sum_ps[rows, q0:HALF], ones[:, :], pt, start=(j == 0), stop=(j == end),
                                        tile_position=(0, h * D))
                last.then_inc(pv_done, 1)

            pe.wait_ge(setup, 4)
            pe.wait_ge(xt_loaded, 16)
            for tile in range(PROJ_TILES):
                for e in range(EC):
                    projection(0, tile, e, tile)
            pe.wait_ge(stacked, 16 * STACK_DMAS)
            for c in range(CHUNKS):
                max_chunk(0, c, c)
            for tile in range(PROJ_TILES):
                for e in range(EC):
                    projection(1, tile, e, PROJ_TILES + tile)
            max_transpose(2 * PROJ_TILES, 1)

            def body(b, last):
                for g in range(NG):
                    n = b * NG + g
                    uses = n * BANK_USES + USES_BEFORE
                    done = 0
                    for u in range(UNITS):
                        if u == 0:
                            pe.wait_ge(max_rows, n * 16 + 16)
                        scores(g % GENS, u, n * UNITS + u)
                        if ahead(g, 1, last) and u >= AHEAD_FROM:
                            if u == AHEAD_FROM:
                                pe.wait_ge(stacked, n * (16 * STACK_DMAS) + 32 * STACK_DMAS)
                            while done < CHUNKS and done < (u - AHEAD_FROM + 1) * 3 // 2:
                                max_chunk((g + 1) % GENS, done, (n + 1) * CHUNKS + done)
                                done += 1
                            if u == MAX_T_AT:
                                max_transpose(uses + (PROJ_TILES if ahead(g, 2, last) else 0), n + 2)
                        if u >= 2:
                            values(g % GENS, u - 2, n * UNITS + u - 2, n * 2 + (0 if u - 2 < HG * EC else 1))
                        if ahead(g, 2, last) and AHEAD_FROM <= u < AHEAD_FROM + PROJ_TILES * EC:
                            tile, e = divmod(u - AHEAD_FROM, EC)
                            if g == 2 and tile == 0 and e == 0:
                                pe.wait_ge(xt_loaded, b * 16 + 32)
                            projection((g + 2) % NG, tile, e, uses + tile)
                    for u in (UNITS - 2, UNITS - 1):
                        values(g % GENS, u, n * UNITS + u, n * 2 + 1)

            batches(pe, body)

        @block.scalar
        def _(act):
            act.sem_inc(exp_done, SCORE_BANKS)
            act.sem_inc(out_copied, 1)

            def body(b, last):
                for g in range(NG):
                    n = b * NG + g
                    for u in range(UNITS):
                        q0 = unit_block(u)[3]
                        count = n * UNITS + u
                        act.wait_ge(scores_ready, count + 1)
                        act.wait_ge(pv_done, count + 1)
                        nc.scalar.activation(probs[:, u % PROB_SLOTS, 0:HALF - q0],
                                             score_ps[:, u % SCORE_BANKS, 0:HALF - q0], ACT.Exp,
                                             scale=exp_scale[:, 0:1]).then_inc(exp_done, 1)
                        for half, at in ((0, COPY_AT), (1, UNITS - 1)):
                            if u == at:
                                end = HG * EC if half == 0 else UNITS
                                act.wait_ge(pv_done, n * UNITS + end + PROB_SLOTS)
                                act.wait_ge(norm_step, (n * 2 + half) * 3 + 3)
                                nc.scalar.activation(o_raw[:, :], out_ps[:, :], ACT.Copy).then_inc(out_copied, 1)

            batches(act, body)

        @block.vector
        def _(dve):
            dve.sem_inc(proj_read, 1)
            dve.sem_inc(chunk_read, MAX_BANKS)
            dve.sem_inc(l_copied, 1)
            dve.sem_inc(norm_step, 3)
            dve.wait_ge(setup, 4)

            def read_projection(gen, tile, uses, group):
                dve.wait_ge(proj_ready, uses + 1)
                if tile < 4:
                    which, half = divmod(tile, 2)
                    if tile == 0 and group is not None:
                        dve.wait_ge(stacked, group * (16 * STACK_DMAS))
                    cols = slice(half * HALF, (half + 1) * HALF)
                    nc.vector.tensor_copy(stage[:, which, 0, cols], proj_ps[:, :]).then_inc(hi_done, 1)
                    dve.wait_ge(hi_done, (0 if group is None else group * 4) + tile + 1)
                    nc.vector.tensor_tensor(stage[:, which, 1, cols], proj_ps[:, :], stage[:, which, 0, cols],
                                            ALU.subtract).then_inc(proj_read, 1)
                else:
                    t0 = (tile - 4) * EC
                    nc.vector.tensor_copy(v[:, gen, t0:t0 + EC, :],
                                          proj_ps[:, :].rearrange("p (t f) -> p t f", t=EC)).then_inc(proj_read, 1)

            def reduce_chunk(c, count):
                h, i, k0, width, _ = chunk_block(c)
                dve.wait_ge(chunk_ready, count + 1)
                nc.vector.tensor_reduce(mx[:, 1 if k0 else 0, h, i:i + 1], max_ps[:, c % MAX_BANKS, 0:width],
                                        AX_X, ALU.max).then_inc(chunk_read, 1)

            def prepare_max(group):
                dve.wait_ge(chunk_read, group * CHUNKS + CHUNKS + MAX_BANKS)
                nc.vector.tensor_tensor(mxall[:, :, :], mx[:, 0], mx[:, 1], ALU.max).then_inc(max_step, 1)
                dve.wait_ge(max_step, group * 3 + 1)
                nc.vector.tensor_scalar(m32[:, :], mxall[:, :, :].rearrange("p h i -> p (h i)"), -1.0 / SHIFT_ROW,
                                        None, ALU.mult).then_inc(max_step, 1)
                dve.wait_ge(max_step, group * 3 + 2)
                nc.vector.tensor_copy(mparts[:, 0], m32[:, :]).then_inc(max_step, 1)
                dve.wait_ge(max_step, group * 3 + 3)
                nc.vector.tensor_tensor(mparts[:, 1], m32[:, :], mparts[:, 0], ALU.subtract).then_inc(max_ready, 1)

            def copy_max_t(uses, group):
                dve.wait_ge(proj_ready, uses + 1)
                if group is not None:
                    dve.wait_ge(max_rows, group * 16)
                nc.vector.tensor_copy(mt[:, :], proj_ps[:, :].bitcast(F16)[0:2 * HG * TT, 0:P]).then_inc(proj_read, 1)

            def copy_sums(n, half):
                dve.wait_ge(pv_done, n * UNITS + (HG * EC if half == 0 else UNITS) + PROB_SLOTS)
                nc.vector.tensor_copy(l_raw[:, :], sum_ps[:, :]).then_inc(l_copied, 1)

            def normalise(n, half):
                k = n * 2 + half
                dve.wait_ge(l_copied, k + 1 + 1)
                nc.vector.reciprocal(l_inv[:, :], l_raw[:, :]).then_inc(norm_step, 1)
                dve.wait_ge(norm_step, k * 3 + 1 + 3)
                dve.wait_ge(out_copied, k + 1 + 1)
                nc.vector.tensor_tensor(o_norm[:, :], o_raw[:, :], l_inv[:, :], ALU.mult).then_inc(norm_step, 1)
                dve.wait_ge(norm_step, k * 3 + 2 + 3)
                dve.wait_ge(o_stored[half], n * 16 + 16)
                nc.vector.tensor_copy(o_part[:, half, 0], o_norm[:, :]).then_inc(norm_step, 1)
                dve.wait_ge(norm_step, k * 3 + 3 + 3)
                nc.vector.tensor_tensor(o_part[:, half, 1], o_norm[:, :], o_part[:, half, 0], ALU.subtract
                                        ).then_inc(o_ready, 1)

            for tile in range(PROJ_TILES):
                read_projection(0, tile, tile, None)
            for c in range(CHUNKS):
                reduce_chunk(c, c)
            prepare_max(0)
            for tile in range(PROJ_TILES):
                read_projection(1, tile, PROJ_TILES + tile, 1)
            copy_max_t(2 * PROJ_TILES, None)

            def body(b, last):
                for g in range(NG):
                    n = b * NG + g
                    uses = n * BANK_USES + USES_BEFORE
                    done = 0
                    for u in range(AHEAD_FROM, UNITS):
                        if ahead(g, 1, last):
                            while done < CHUNKS and done < (u - AHEAD_FROM + 1) * 3 // 2:
                                reduce_chunk(done, (n + 1) * CHUNKS + done)
                                done += 1
                                if done == CHUNKS:
                                    prepare_max(n + 1)
                            if u == MAX_T_AT:
                                copy_max_t(uses + (PROJ_TILES if ahead(g, 2, last) else 0), n + 1)
                        if u == COPY_AT:
                            copy_sums(n, 0)
                        if ahead(g, 2, last) and u < AHEAD_FROM + PROJ_TILES * EC:
                            tile, e = divmod(u - AHEAD_FROM, EC)
                            if e == EC - 1:
                                read_projection((g + 2) % GENS, tile, uses + tile, n + 2)
                        if u == COPY_AT + 3:
                            normalise(n, 0)
                    copy_sums(n, 1)
                    normalise(n, 1)

            batches(dve, body)


GATES = 3
STEPS = 4


def recurrence(nc, xt_dram, w_gates, u_gates, inv, bias, c_start, c_scale, c_parts):
    with ExitStack() as ctx:
        def sb(name, shape, dt):
            return ctx.enter_context(nc.sbuf_tensor(f"rc_{name}", shape, dt))

        def sem(name):
            return ctx.enter_context(nc.semaphore(f"rc_{name}"))

        xt = sb("xt", [P, 2, HL, EC, HALF], F16)
        c = sb("c", [P, 2, EC, HALF], F32)
        act_out = sb("act_out", [P, 2, GATES, HALF], F32)
        fc = sb("fc", [P, HALF], F32)
        ig = sb("ig", [P, HALF], F32)
        total = sb("total", [P, HALF], F32)
        halfscale = sb("halfscale", [P, GATES, EC], F32)
        halfbias = sb("halfbias", [P, GATES, EC], F32)
        z = ctx.enter_context(nc.psum_tensor("rc_z", [P, 2 * GATES, HALF], F32))
        x_loaded, z_ready, z_read = [sem("x_loaded0"), sem("x_loaded1")], sem("z_ready"), sem("z_read")
        own, c_ready, consts = sem("own"), sem("c_ready"), sem("consts")
        block = ctx.enter_context(nc.Block())
        ROUND = EC * STEPS
        FACTOR = (0.5, 0.5, 1.0)

        @block.sync
        def _(sp):
            with sp.Fori(0, B // 2) as i:
                for s in range(STEPS):
                    t, half = divmod(s, 2)
                    sp.wait_ge(z_ready, i * (ROUND * GATES) + (s + 1) * EC * GATES)
                    sp.dma_start(xt[:, s % 2],
                                 xt_dram[bass.ds(i * 2 + t, 1), :, :, :, half * HALF:(half + 1) * HALF]
                                 .rearrange("o p l e t -> p (o l) e t")).then_inc(x_loaded[s % 2], 16)

        @block.tensor
        def _(pe):
            pe.sem_inc(z_ready, 2 * EC * GATES)
            with pe.Fori(0, B // 2) as i:
                for s in range(STEPS):
                    t, half = divmod(s, 2)
                    pe.wait_ge(x_loaded[s % 2], i * (8 * STEPS) + 16 * (s // 2 + 1))
                    for m in range(EC):
                        k = s * EC + m
                        for gate in range(GATES):
                            bank = z[:, (k % 2) * GATES + gate]
                            pe.wait_ge(z_read, i * (ROUND * GATES) + k * GATES + gate + 1)
                            for q, (a, l) in enumerate(PASSES):
                                for e in range(EC):
                                    nc.tensor.matmul(bank, w_gates[:, a, e, gate * E + m * P:gate * E + (m + 1) * P],
                                                     xt[:, s % 2, l, e, :], start=(q == 0 and e == 0), stop=False)
                            if m == 0 and gate == 0:
                                pe.wait_ge(c_ready, i * ROUND + s * EC + EC)
                            for q, (a, l) in enumerate(PASSES):
                                for e in range(EC):
                                    last = nc.tensor.matmul(
                                        bank, u_gates[:, a, e, gate * E + m * P:gate * E + (m + 1) * P],
                                        c_parts[:, half, t, l, e, :], start=False,
                                        stop=(q == len(PASSES) - 1 and e == EC - 1))
                            last.then_inc(z_ready, 1)

        @block.scalar
        def _(act):
            act.sem_inc(z_read, 2 * GATES)
            act.wait_ge(consts, GATES * 2)
            with act.Fori(0, B // 2) as i:
                for s in range(STEPS):
                    for m in range(EC):
                        k = s * EC + m
                        act.wait_ge(c_ready, i * ROUND + k + 7)
                        for gate in range(GATES):
                            act.wait_ge(z_ready, i * (ROUND * GATES) + k * GATES + gate + 1 + 2 * EC * GATES)
                            nc.scalar.activation(act_out[:, k % 2, gate], z[:, (k % 2) * GATES + gate], ACT.Tanh,
                                                 bias=halfbias[:, gate, m:m + 1],
                                                 scale=halfscale[:, gate, m:m + 1]).then_inc(z_read, 1)

        @block.vector
        def _(dve):
            for gate in range(GATES):
                nc.vector.tensor_scalar(halfscale[:, gate], inv[:, gate], FACTOR[gate], None, ALU.mult
                                        ).then_inc(consts, 1)
                nc.vector.tensor_scalar(halfbias[:, gate], bias[:, gate], FACTOR[gate], None, ALU.mult
                                        ).then_inc(consts, 1)
            ch = Chain(dve, own)
            for half in range(2):
                for m in range(EC):
                    ch.after(nc.vector.tensor_copy(c[:, half, m], c_start[:, m:m + 1].broadcast_to([P, HALF])))
                    ch.after(nc.vector.tensor_scalar(c_parts[:, half, 0, 0, m], c[:, half, m], c_scale[:, 0:1], None,
                                                     ALU.mult))
                    nc.vector.scalar_tensor_tensor(c_parts[:, half, 0, 1, m], c[:, half, m], c_scale[:, 0:1],
                                                   c_parts[:, half, 0, 0, m], ALU.mult, ALU.subtract
                                                   ).then_inc(c_ready, 1)
            before = ch.count
            LINKS = 5
            with dve.Fori(0, B // 2) as i:
                ch = Chain(dve, own, i * (ROUND * LINKS) + before)
                for s in range(STEPS):
                    t, half = divmod(s, 2)
                    for m in range(EC):
                        k = s * EC + m
                        dve.wait_ge(z_read, i * (ROUND * GATES) + (k + 1) * GATES + 2 * GATES)
                        f, g_in, g_cell = (act_out[:, k % 2, gate] for gate in range(GATES))
                        new = c_parts[:, half, 1 - t]
                        ch.after(nc.vector.scalar_tensor_tensor(fc[:, :], f, 1.0, c[:, half, m], ALU.add, ALU.mult))
                        ch.after(nc.vector.scalar_tensor_tensor(ig[:, :], g_in, 1.0, g_cell, ALU.add, ALU.mult))
                        ch.after(nc.vector.tensor_tensor(total[:, :], fc[:, :], ig[:, :], ALU.add))
                        ch.after(nc.vector.tensor_scalar(c[:, half, m], total[:, :], 0.5, None, ALU.mult))
                        ch.after(nc.vector.tensor_scalar(new[:, 0, m], c[:, half, m], c_scale[:, 0:1], None, ALU.mult))
                        nc.vector.scalar_tensor_tensor(new[:, 1, m], c[:, half, m], c_scale[:, 0:1], new[:, 0, m],
                                                       ALU.mult, ALU.subtract).then_inc(c_ready, 1)


def output_layer(nc, xt_dram, x1, out, w_o, u_o, inv_dram, bo, c_parts):
    with ExitStack() as ctx:
        def sb(name, shape, dt):
            return ctx.enter_context(nc.sbuf_tensor(f"ol_{name}", shape, dt))

        def sem(name):
            return ctx.enter_context(nc.semaphore(f"ol_{name}"))

        def slots(name):
            return [sem(f"{name}{s}") for s in range(2)]

        xt = sb("xt", [P, 2, HL, EC, T], F16)
        res = sb("res", [P, 2, TT, E], F32)
        state = sb("state", [P, TT, E], F32)
        scaled = sb("scaled", [P, 2, E], F32)
        summed = sb("summed", [P, 2, E], F32)
        h = sb("h", [P, 2, E], F32)
        inv_row = sb("inv_row", [P, E], F32)
        bo_row = sb("bo_row", [P, E], F32)
        z = ctx.enter_context(nc.psum_tensor("ol_z", [P, 4, E], F32))
        rows, x_loaded, res_loaded = sem("rows"), slots("x_loaded"), slots("res_loaded")
        z_ready, z_read, summed_ready, h_ready = sem("z_ready"), sem("z_read"), sem("summed_ready"), sem("h_ready")
        done, stored = sem("done"), slots("stored")
        block = ctx.enter_context(nc.Block())
        BANKS = 4

        @block.sync
        def _(sp):
            sp.dma_start(inv_row[:, :], inv_dram.partition_broadcast(P)).then_inc(rows, 16)
            sp.dma_start(bo_row[:, :], bo.partition_broadcast(P)).then_inc(rows, 16)
            def load(b, s):
                sp.dma_start(xt[:, s], xt_dram[bass.ds(b, 1)].rearrange("o p l e t -> p (o l) e t")
                             ).then_inc(x_loaded[s], 16)
                sp.dma_start(res[:, s], x1[bass.ds(b, 1)].rearrange("o (t p) e -> p (o t) e", p=P)
                             ).then_inc(res_loaded[s], 16)

            def pair(i, last):
                for s in range(2):
                    if not (last and s == 1):
                        sp.wait_ge(stored[1 - s], i * 16 + (16 if s == 0 else 32))
                        load(i * 2 + s + 1, 1 - s)
                    sp.wait_ge(done, i * (2 * TT) + (s + 1) * TT)
                    sp.dma_start(out[bass.ds(i * 2 + s, 1)].rearrange("o (t p) e -> p (o t) e", p=P), res[:, s]
                                 ).then_inc(stored[s], 16)

            for s in range(2):
                sp.sem_inc(stored[s], 16)
            load(0, 0)
            with sp.Fori(0, B // 2 - 1) as i:
                pair(i, False)
            pair(B // 2 - 1, True)
            for s in range(2):
                sp.wait_ge(stored[s], 16 * (B // 2) + 16)

        @block.tensor
        def _(pe):
            for n in range(TT):
                half, col = divmod(n, EC)
                if n >= BANKS:
                    pe.wait_ge(z_read, n - BANKS + 1)
                for q, (a, l) in enumerate(PASSES):
                    for e in range(EC):
                        last = nc.tensor.matmul(z[:, n % BANKS], c_parts[:, half, 0, a, e, col * P:(col + 1) * P],
                                                u_o[:, l, e, :], start=(q == 0 and e == 0),
                                                stop=(q == len(PASSES) - 1 and e == EC - 1))
                last.then_inc(z_ready, 1)
            with pe.Fori(0, B // 2) as i:
                for s in range(2):
                    pe.wait_ge(x_loaded[s], i * 16 + 16)
                    for t in range(TT):
                        n = i * (2 * TT) + s * TT + t + TT
                        pe.wait_ge(z_read, n - BANKS + 1)
                        for q, (a, l) in enumerate(PASSES):
                            for e in range(EC):
                                last = nc.tensor.matmul(z[:, t % BANKS], xt[:, s, a, e, t * P:(t + 1) * P],
                                                        w_o[:, l, e, :], start=(q == 0 and e == 0),
                                                        stop=(q == len(PASSES) - 1 and e == EC - 1))
                        last.then_inc(z_ready, 1)

        @block.scalar
        def _(act):
            with act.Fori(0, B // 2) as i:
                for s in range(2):
                    for t in range(TT):
                        n = i * (2 * TT) + s * TT + t
                        act.wait_ge(summed_ready, n + TT + 1)
                        nc.scalar.activation(h[:, t % 2], summed[:, t % 2], ACT.Tanh).then_inc(h_ready, 1)

        @block.vector
        def _(dve):
            dve.wait_ge(rows, 32)
            for n in range(TT):
                dve.wait_ge(z_ready, n + 1)
                nc.vector.tensor_tensor(scaled[:, n % 2], z[:, n % BANKS], inv_row[:, :], ALU.mult).then_inc(z_read, 1)
                dve.wait_ge(z_read, n + 1)
                nc.vector.tensor_tensor(state[:, n], scaled[:, n % 2], bo_row[:, :], ALU.add).then_inc(summed_ready, 1)
            dve.wait_ge(summed_ready, TT)
            with dve.Fori(0, B // 2) as i:
                for s in range(2):
                    dve.wait_ge(res_loaded[s], i * 16 + 16)

                    def residual(i, s, t):
                        n = i * (2 * TT) + s * TT + t
                        dve.wait_ge(h_ready, n + 1)
                        nc.vector.tensor_tensor(res[:, s, t], res[:, s, t], h[:, t % 2], ALU.add).then_inc(done, 1)

                    for t in range(TT):
                        n = i * (2 * TT) + s * TT + t + TT
                        dve.wait_ge(z_ready, n + 1)
                        nc.vector.tensor_tensor(scaled[:, t % 2], z[:, t % BANKS], inv_row[:, :], ALU.mult
                                                ).then_inc(z_read, 1)
                        dve.wait_ge(z_read, n + 1)
                        if t >= 2:
                            residual(i, s, t - 2)
                        nc.vector.tensor_tensor(summed[:, t % 2], scaled[:, t % 2], state[:, t], ALU.add
                                                ).then_inc(summed_ready, 1)
                    residual(i, s, TT - 2)
                    residual(i, s, TT - 1)


def build(nc, x, w_in, w_out, wf, uf, bf, wi, ui, bi, wc, uc, bc, wo, uo, bo, in_c, out):
    def scratch(name, shape, dt):
        return nc.dram_tensor(name, shape, dt, kind="Internal").ap()

    xt1 = scratch("xt1", (B, P, HL, EC, T), F16)
    xt2 = scratch("xt2", (B, P, HL, EC, T), F16)
    ot = scratch("ot", (B, P, HL, NG, T), F16)
    x1 = scratch("x1", (B, T, E), F32)
    m_dram = scratch("m_dram", (2, HG, T), F16)
    v_row = scratch("v_row", (E,), F32)
    out_row = scratch("out_row", (E,), F32)
    o_row = scratch("o_row", (E,), F32)
    with ExitStack() as ctx:
        ctx.enter_context(nc.allow_non_contiguous_dma(reason="a few vectors of 512 numbers, spread over the partitions"))

        def sb(name, shape, dt, c=ctx):
            return c.enter_context(nc.sbuf_tensor(name, shape, dt))

        ident16 = sb("ident16", [P, P], F16)
        identb = sb("identb", [P, P], BF16)
        neg_m = sb("neg_m", [P, P], BF16)
        neg_s = sb("neg_s", [P, P], BF16)
        bias = sb("bias", [P, GATES, EC], F32)
        c_start = sb("c_start", [P, EC], F32)
        c_row = sb("c_row", [P, E], F32)
        c_top = sb("c_top", [P, 1], F32)
        c_inv = sb("c_inv", [P, 1], F32)
        c_scale = sb("c_scale", [P, 1], F32)
        exp_scale = sb("exp_scale", [P, 1], F32)

        with nc.semaphore("made") as made, nc.semaphore("consts_in") as consts_in, nc.semaphore("c_steps") as c_steps, \
                nc.Block() as block:
            @block.sync
            def _(sp):
                for g, v in enumerate((bf, bi, bc)):
                    sp.dma_start(bias[:, g, :], v.rearrange("(t p) -> p t", p=P)).then_inc(consts_in, 16)
                sp.dma_start(c_start[:, :], in_c.rearrange("(t p) -> p t", p=P)).then_inc(consts_in, 16)
                sp.dma_start(c_row[:, :], in_c.partition_broadcast(P)).then_inc(consts_in, 16)

            @block.gpsimd
            def _(pool):
                for tile, value in ((ident16, 0.0), (identb, 0.0), (neg_m, 0.0), (neg_s, 0.0)):
                    nc.gpsimd.memset(tile[:, :], value).then_inc(made, 1)
                pool.wait_ge(made, 4)
                for tile in (ident16, identb):
                    nc.gpsimd.affine_select(out=tile[:, :], in_=tile[:, :], compare_op=ALU.not_equal, fill=1.0, base=0,
                                            pattern=[[-1, P]], channel_multiplier=1)
                nc.gpsimd.affine_select(out=neg_m[:, :], in_=neg_m[:, :], compare_op=ALU.is_ge, fill=MASKED, base=0,
                                        pattern=[[-1, P]], channel_multiplier=1)
                nc.gpsimd.affine_select(out=neg_s[:, :], in_=neg_s[:, :], compare_op=ALU.is_ge, fill=MASKED, base=0,
                                        pattern=[[1, P]], channel_multiplier=-1).then_inc(made, 1)
                pool.wait_ge(made, 5)

            @block.vector
            def _(dve):
                ch = Chain(dve, c_steps)
                dve.wait_ge(consts_in, 80)
                ch.after(nc.vector.tensor_reduce(c_top[:, :], c_row[:, :], AX_X, ALU.max, apply_absolute_value=True))
                ch.after(nc.vector.tensor_scalar(c_inv[:, :], c_top[:, :], 1.0, None, ALU.max))
                ch.after(nc.vector.tensor_scalar(c_inv[:, :].bitcast(U32), c_inv[:, :].bitcast(U32), EXPONENT, None,
                                                 ALU.bitwise_and))
                ch.after(nc.vector.reciprocal(c_scale[:, :], c_inv[:, :]))

        with ExitStack() as first:
            w_qkv = sb("w_qkv", [P, HL, EC, 3 * E], F16, first)
            w_o1 = sb("w_o1", [P, HL, EC, E], F16, first)
            inv1 = sb("inv1", [P, 4, EC], F32, first)
            prepare_weights(nc, "pa", [[(w_in[2 * E:3 * E], w_qkv, 2 * E)], [(w_in[0:E], w_qkv, 0)],
                                       [(w_in[E:2 * E], w_qkv, E)], [(w_out, w_o1, 0)]],
                            inv1, ident16, (1, 2), scratch_v=(0, v_row))
            with nc.semaphore("row_out") as row_out, nc.semaphore("scale_set") as scale_set, nc.Block() as block:
                @block.sync
                def _(sp):
                    sp.dma_start(out_row.rearrange("(t p) -> p t", p=P), inv1[:, 3, :]).then_inc(row_out, 16)
                    sp.wait_ge(row_out, 16)

                @block.vector
                def _(dve):
                    nc.vector.scalar_tensor_tensor(exp_scale[:, :], inv1[:, 1, 0:1], D ** -0.5, inv1[:, 2, 0:1],
                                                   ALU.mult, ALU.mult).then_inc(scale_set, 1)
                    dve.wait_ge(scale_set, 1)
            normalise_tokens(nc, "n1", x, xt1, ident16)
            attention(nc, xt1, ot, m_dram, w_qkv, exp_scale, ident16, identb, neg_m, neg_s)
            normalise_tokens(nc, "n2", x, xt2, ident16, outproj=(ot, w_o1, out_row, x1))

        w_gates = sb("w_gates", [P, HL, EC, GATES * E], F16)
        u_gates = sb("u_gates", [P, HL, EC, GATES * E], F16)
        w_o = sb("w_o", [P, HL, EC, E], F16)
        u_o = sb("u_o", [P, HL, EC, E], F16)
        inv2 = sb("inv2", [P, 4, EC], F32)
        c_parts = sb("c_parts", [P, 2, 2, HL, EC, HALF], F16)
        prepare_weights(nc, "pb", [[(w, w_gates, g * E), (u, u_gates, g * E)]
                                   for g, (w, u) in enumerate(((wf, uf), (wi, ui), (wc, uc)))] +
                        [[(wo, w_o, 0), (uo, u_o, 0)]], inv2, ident16, (), c_scale=c_inv)
        with nc.semaphore("row_out2") as row_out2, nc.Block() as block:
            @block.sync
            def _(sp):
                sp.dma_start(o_row.rearrange("(t p) -> p t", p=P), inv2[:, 3, :]).then_inc(row_out2, 16)
                sp.wait_ge(row_out2, 16)
        recurrence(nc, xt2, w_gates, u_gates, inv2, bias, c_start, c_scale, c_parts)
        output_layer(nc, xt2, x1, out, w_o, u_o, o_row, bo, c_parts)


INS = ("L0_attn_query", "L0_attn_in_proj_weight", "L0_attn_out_proj_weight", "L0_ffn_wf", "L0_ffn_uf", "L0_ffn_bf",
       "L0_ffn_wi", "L0_ffn_ui", "L0_ffn_bi", "L0_ffn_wc", "L0_ffn_uc", "L0_ffn_bc", "L0_ffn_wo", "L0_ffn_uo",
       "L0_ffn_bo", "L0_ffn_in_c")


def kernel(**inputs):
    import numpy as _np
    import concourse.bacc as _bacc
    from concourse import mybir as _mybir
    from concourse.bass_utils import run_bass_kernel_spmd as _run

    nc = _bacc.Bacc("TRN2", target_bir_lowering=False, num_devices=1)
    arrays, args = {}, []
    for name in INS:
        a = _np.ascontiguousarray(inputs[name])
        arrays[f"in_{name}"] = a
        args.append(nc.dram_tensor(f"in_{name}", a.shape, _mybir.dt.from_np(a.dtype), kind="ExternalInput").ap())
    args.append(nc.dram_tensor("out_0", (B, T, E), F32, kind="ExternalOutput").ap())
    nc.disable_value_cache = True
    build(nc, *args)
    r = _run(nc, [arrays], core_ids=[0])
    return r.results[0]["out_0"]
```

```python
from contextlib import ExitStack

import concourse.bass as bass
from concourse import mybir

ALU = mybir.AluOpType
ACT = mybir.ActivationFunctionType
AX_X = mybir.AxisListType.X
F32 = mybir.dt.float32
F16 = mybir.dt.float16
BF16 = mybir.dt.bfloat16
U32 = mybir.dt.uint32
POOL_MAX = bass.bass_isa.ReduceOp.max

P = 128
B, T, E = 8, 1024, 512
H, D = 16, 32
TT = T // P
EC = E // P
HG = P // D
NG = H // HG
HALF = T // 2
LN_EPS = 1e-5
HL = 2
EXPONENT = 0x7F800000
W_TOP = 4.0
SHIFT_ROW = 32768.0
MASKED = -3.0e38
PASSES = ((0, 0), (0, 1), (1, 0))


class Chain:

    def __init__(self, eng, sem, base=0):
        self.eng, self.sem, self.base, self.count = eng, sem, base, 0

    def after(self, instruction):
        instruction.then_inc(self.sem, 1)
        self.count += 1
        self.eng.wait_ge(self.sem, self.base + self.count)


def prepare_weights(nc, tag, jobs, inv, ident16, global_rows, scratch_v=None, c_scale=None):
    J = len(jobs)
    M = max(len(j) for j in jobs)
    with ExitStack() as ctx:
        def sb(name, shape, dt):
            return ctx.enter_context(nc.sbuf_tensor(f"{tag}_{name}", shape, dt))

        def sem(name):
            return ctx.enter_context(nc.semaphore(f"{tag}_{name}"))

        nat = sb("nat", [P, 2, M * EC, E], F32)
        part = sb("part", [P, 2, HL, M * EC, E], F16)
        rowmax = sb("rowmax", [P, M * EC], F32)
        pairmax = sb("pairmax", [P, EC], F32)
        onemax = sb("onemax", [P, 1], F32)
        allmax = sb("allmax", [P, 1], F32)
        scale = sb("scale", [P, EC], F32)
        vrow = sb("vrow", [P, E], F32)
        tp = ctx.enter_context(nc.psum_tensor(f"{tag}_tp", [P, 4, HL * EC * P], F16))
        loaded, nat_used = [sem("loaded0"), sem("loaded1")], sem("nat_used")
        transposed, evacuated, own = sem("transposed"), sem("evacuated"), sem("own")
        max_in, max_out = sem("max_in"), sem("max_out")
        vinv_ready, vinv_stored, vinv_loaded = sem("vinv_ready"), sem("vinv_stored"), sem("vinv_loaded")
        block = ctx.enter_context(nc.Block())

        loads_until = [16 * sum(len(other) for other in jobs[j % 2:j + 1:2]) for j in range(J)]
        tiles_until = [0]
        for job in jobs:
            tiles_until.append(tiles_until[-1] + len(job) * EC)

        @block.sync
        def _(sp):
            for j, job in enumerate(jobs):
                if j >= 2:
                    sp.wait_ge(nat_used, j - 1)
                for m, (w, _, _) in enumerate(job):
                    sp.dma_start(nat[:, j % 2, m * EC:(m + 1) * EC, :],
                                 w.rearrange("(t p) e -> p t e", p=P)).then_inc(loaded[j % 2], 16)
            if scratch_v is not None:
                v_job, row = scratch_v
                sp.wait_ge(vinv_ready, 1)
                sp.dma_start(row.rearrange("(t p) -> p t", p=P), inv[:, v_job, :]).then_inc(vinv_stored, 16)
                sp.wait_ge(vinv_stored, 16)
                sp.dma_start(vrow[:, :], row.partition_broadcast(P)).then_inc(vinv_loaded, 16)

        @block.gpsimd
        def _(pool):
            for k in range(len(global_rows)):
                pool.wait_ge(max_in, k + 1)
                nc.gpsimd.partition_all_reduce(allmax[:, :], onemax[:, :], P, POOL_MAX).then_inc(max_out, 1)

        @block.vector
        def _(dve):
            ch = Chain(dve, own)
            n_global = 0
            for j, job in enumerate(jobs):
                m = len(job)
                w = nat[:, j % 2]
                dve.wait_ge(loaded[j % 2], loads_until[j])
                if scratch_v is not None and j == J - 1:
                    dve.wait_ge(vinv_loaded, 16)
                    ch.after(nc.vector.tensor_tensor(w[:, 0:EC, :], w[:, 0:EC, :],
                                                     vrow[:, :].unsqueeze(1).broadcast_to([P, EC, E]), ALU.mult))
                if c_scale is not None and m == 2:
                    ch.after(nc.vector.tensor_scalar(w[:, EC:2 * EC, :], w[:, EC:2 * EC, :],
                                                     c_scale[:, 0:1], None, ALU.mult))
                ch.after(nc.vector.tensor_reduce(rowmax[:, 0:m * EC], w[:, 0:m * EC, :], AX_X, ALU.max,
                                                 apply_absolute_value=True))
                top = rowmax[:, 0:EC]
                if m == 2:
                    ch.after(nc.vector.tensor_tensor(pairmax[:, :], rowmax[:, 0:EC], rowmax[:, EC:2 * EC], ALU.max))
                    top = pairmax[:, :]
                if j in global_rows:
                    ch.after(nc.vector.tensor_reduce(onemax[:, :], top, AX_X, ALU.max))
                    n_global += 1
                    nc.vector.engine_nop().then_inc(max_in, 1)
                    dve.wait_ge(max_out, n_global)
                    top = allmax[:, 0:1].broadcast_to([P, EC])
                ch.after(nc.vector.tensor_scalar(scale[:, :], top, 1e-15, None, ALU.max))
                ch.after(nc.vector.tensor_scalar(scale[:, :].bitcast(U32), scale[:, :].bitcast(U32),
                                                 EXPONENT, None, ALU.bitwise_and))
                ch.after(nc.vector.tensor_scalar(inv[:, j, :], scale[:, :], 1.0 / W_TOP, None, ALU.mult))
                if scratch_v is not None and j == scratch_v[0]:
                    nc.vector.engine_nop().then_inc(vinv_ready, 1)
                ch.after(nc.vector.reciprocal(scale[:, :], inv[:, j, :]))
                if j >= 2:
                    dve.wait_ge(transposed, tiles_until[j - 1])
                for k in range(m):
                    ws = w[:, k * EC:(k + 1) * EC, :]
                    ch.after(nc.vector.tensor_tensor(ws, ws, scale[:, :].unsqueeze(2).broadcast_to([P, EC, E]),
                                                     ALU.mult))
                    hi = part[:, j % 2, 0, k * EC:(k + 1) * EC, :]
                    lo = part[:, j % 2, 1, k * EC:(k + 1) * EC, :]
                    ch.after(nc.vector.tensor_copy(hi, ws))
                    last = nc.vector.tensor_tensor(lo, ws, hi, ALU.subtract)
                    if k == m - 1:
                        last.then_inc(nat_used, 1)
                    else:
                        ch.after(last)

        @block.tensor
        def _(pe):
            n = 0
            for j, job in enumerate(jobs):
                pe.wait_ge(nat_used, j + 1)
                for k in range(len(job) * EC):
                    if n >= 4:
                        pe.wait_ge(evacuated, n - 3)
                    for hl in range(HL):
                        for e in range(EC):
                            last = nc.tensor.transpose(tp[:, n % 4, (hl * EC + e) * P:(hl * EC + e + 1) * P],
                                                       part[:, j % 2, hl, k, e * P:(e + 1) * P], ident16[:, :])
                    last.then_inc(transposed, 1)
                    n += 1

        @block.scalar
        def _(act):
            n = 0
            for job in jobs:
                for _, target, col in job:
                    for t in range(EC):
                        act.wait_ge(transposed, n + 1)
                        nc.scalar.activation(
                            target[:, :, :, col + t * P:col + (t + 1) * P],
                            tp[:, n % 4, :].rearrange("p (l e f) -> p l e f", l=HL, e=EC),
                            ACT.Copy).then_inc(evacuated, 1)
                        n += 1


def normalise_tokens(nc, tag, src, dst_t, ident16, outproj=None):
    with ExitStack() as ctx:
        def sb(name, shape, dt):
            return ctx.enter_context(nc.sbuf_tensor(f"{tag}_{name}", shape, dt))

        def sem(name):
            return ctx.enter_context(nc.semaphore(f"{tag}_{name}"))

        def slots(name):
            return [sem(f"{name}{s}") for s in range(2)]

        x = sb("x", [P, 2, TT, E], F32)
        xh = sb("xh", [P, 2, E], F32)
        hi = sb("hi", [P, 2, E], F16)
        lo = sb("lo", [P, 2, E], F16)
        stats = sb("stats", [P, TT, 6], F32)
        mean2, diff, dev = (sb(name, [P, TT], F32) for name in ("mean2", "diff", "dev"))
        diff2, dev_all = (sb(name, [P, TT], F32) for name in ("diff2", "dev_all"))
        var = sb("var", [P, TT], F32)
        std = sb("std", [P, TT], F32)
        rstd = sb("rstd", [P, TT], F32)
        shift = sb("shift", [P, TT], F32)
        xt = sb("xt", [P, 2, HL, EC, T], F16)
        tp = ctx.enter_context(nc.psum_tensor(f"{tag}_tp", [P, 4, HL * EC * P], F16))
        loaded, lo_ready, xh_ready = slots("loaded"), sem("lo_ready"), sem("xh_ready")
        stats_ready, moment, var_ready = sem("stats_ready"), sem("moment"), sem("var_ready")
        std_ready, inverse_ready, rstd_ready = sem("std_ready"), sem("inverse_ready"), sem("rstd_ready")
        hi_ready, transposed, evacuated, stored = sem("hi_ready"), sem("transposed"), sem("evacuated"), slots("stored")
        if outproj:
            o_parts, w_out, inv_out, x1 = outproj
            ot = sb("ot", [P, 2, HL, NG, T], F16)
            y = sb("y", [P, 2, E], F32)
            inv_row = sb("inv_row", [P, E], F32)
            yp = ctx.enter_context(nc.psum_tensor(f"{tag}_yp", [P, 4, E], F32))
            o_loaded, y_ready, y_read = slots("o_loaded"), sem("y_ready"), sem("y_read")
            x1_ready, x1_stored, row_loaded = sem("x1_ready"), slots("x1_stored"), sem("row_loaded")
        block = ctx.enter_context(nc.Block())
        X_CREDIT, TP_CREDIT, PART_CREDIT, Y_CREDIT, STORE_CREDIT = TT, 4, 2, 4, 16

        @block.sync
        def _(sp):
            for s in range(2):
                sp.sem_inc(stored[s], STORE_CREDIT)
                if outproj:
                    sp.sem_inc(x1_stored[s], STORE_CREDIT)
            if outproj:
                sp.dma_start(inv_row[:, :], inv_out.partition_broadcast(P)).then_inc(row_loaded, 16)

            def load(b, s):
                sp.dma_start(x[:, s], src[bass.ds(b, 1)].rearrange("o (t p) e -> p (o t) e", p=P)
                             ).then_inc(loaded[s], 16)
                if outproj:
                    sp.dma_start(ot[:, s], o_parts[bass.ds(b * NG, NG)].rearrange("g p l t -> p l g t")
                                 ).then_inc(o_loaded[s], 16)

            def pair(i, last):
                for s in range(2):
                    b = i * 2 + s
                    if not (last and s == 1):
                        sp.wait_ge(lo_ready, i * (2 * TT) + s * TT + TT)
                        if outproj:
                            sp.wait_ge(x1_stored[1 - s], i * 16 + (STORE_CREDIT if s == 0 else 16 + STORE_CREDIT))
                        load(b + 1, 1 - s)
                    if outproj:
                        sp.wait_ge(x1_ready, i * (2 * TT) + (s + 1) * TT)
                        sp.dma_start(x1[bass.ds(b, 1)].rearrange("o (t p) e -> p (o t) e", p=P), x[:, s]
                                     ).then_inc(x1_stored[s], 16)
                    sp.wait_ge(evacuated, i * (2 * TT) + (s + 1) * TT + TP_CREDIT)
                    sp.dma_start(dst_t[bass.ds(b, 1)].rearrange("o p l e t -> p (o l) e t"), xt[:, s]
                                 ).then_inc(stored[s], 16)

            load(0, 0)
            with sp.Fori(0, B // 2 - 1) as i:
                pair(i, False)
            pair(B // 2 - 1, True)
            for s in range(2):
                sp.wait_ge(stored[s], 16 * (B // 2) + STORE_CREDIT)
                if outproj:
                    sp.wait_ge(x1_stored[s], 16 * (B // 2) + STORE_CREDIT)

        @block.vector
        def _(dve):
            dve.sem_inc(lo_ready, X_CREDIT)
            if outproj:
                dve.sem_inc(y_read, Y_CREDIT)
                dve.wait_ge(row_loaded, 16)
            with dve.Fori(0, B // 2) as i:
                for s in range(2):
                    n = i * (2 * TT) + s * TT
                    dve.wait_ge(loaded[s], i * 16 + 16)
                    for t in range(TT):
                        if outproj:
                            dve.wait_ge(y_ready, n + t + 1)
                            nc.vector.tensor_tensor(y[:, t % 2], yp[:, t % 4], inv_row[:, :], ALU.mult
                                                    ).then_inc(y_read, 1)
                            dve.wait_ge(y_read, n + t + 1 + Y_CREDIT)
                            nc.vector.tensor_tensor(x[:, s, t], x[:, s, t], y[:, t % 2], ALU.add
                                                    ).then_inc(x1_ready, 1)
                            dve.wait_ge(x1_ready, n + t + 1)
                        nc.vector.bn_stats(stats[:, t], x[:, s, t]).then_inc(stats_ready, 1)
                    dve.wait_ge(stats_ready, n + TT)
                    step = i * 10 + s * 5
                    nc.vector.tensor_tensor(mean2[:, :], stats[:, :, 1], stats[:, :, 4], ALU.add).then_inc(moment, 1)
                    nc.vector.tensor_tensor(diff[:, :], stats[:, :, 1], stats[:, :, 4], ALU.subtract).then_inc(moment, 1)
                    nc.vector.tensor_tensor(dev[:, :], stats[:, :, 2], stats[:, :, 5], ALU.add).then_inc(moment, 1)
                    dve.wait_ge(moment, step + 3)
                    nc.vector.tensor_tensor(diff2[:, :], diff[:, :], diff[:, :], ALU.mult).then_inc(moment, 1)
                    dve.wait_ge(moment, step + 4)
                    nc.vector.scalar_tensor_tensor(dev_all[:, :], diff2[:, :], E / 4.0, dev[:, :], ALU.mult, ALU.add
                                                   ).then_inc(moment, 1)
                    dve.wait_ge(moment, step + 5)
                    nc.vector.tensor_scalar(var[:, :], dev_all[:, :], 1.0 / E, LN_EPS, ALU.mult, ALU.add
                                            ).then_inc(var_ready, 1)
                    dve.wait_ge(std_ready, i * 2 + s + 1)
                    nc.vector.reciprocal(rstd[:, :], std[:, :]).then_inc(inverse_ready, 1)
                    dve.wait_ge(inverse_ready, i * 2 + s + 1)
                    nc.vector.scalar_tensor_tensor(shift[:, :], mean2[:, :], -0.5, rstd[:, :],
                                                   ALU.mult, ALU.mult).then_inc(rstd_ready, 1)
                    dve.wait_ge(rstd_ready, i * 2 + s + 1)
                    for t in range(TT):
                        nc.vector.tensor_scalar(xh[:, t % 2], x[:, s, t], rstd[:, t:t + 1], shift[:, t:t + 1],
                                                ALU.mult, ALU.add).then_inc(xh_ready, 1)
                        dve.wait_ge(xh_ready, n + t + 1)
                        dve.wait_ge(hi_ready, n + t + 1)
                        nc.vector.tensor_tensor(lo[:, t % 2], xh[:, t % 2], hi[:, t % 2], ALU.subtract
                                                ).then_inc(lo_ready, 1)

        @block.scalar
        def _(act):
            act.sem_inc(evacuated, TP_CREDIT)

            def evacuate(i, s, t):
                k = i * (2 * TT) + s * TT + t
                act.wait_ge(transposed, k + 1 + PART_CREDIT)
                nc.scalar.activation(xt[:, s, :, :, t * P:(t + 1) * P],
                                     tp[:, t % 4, :].rearrange("p (l e f) -> p l e f", l=HL, e=EC),
                                     ACT.Copy).then_inc(evacuated, 1)

            with act.Fori(0, B // 2) as i:
                for s in range(2):
                    n = i * (2 * TT) + s * TT
                    act.wait_ge(var_ready, i * 2 + s + 1)
                    nc.scalar.activation(std[:, :], var[:, :], ACT.Sqrt).then_inc(std_ready, 1)
                    act.wait_ge(stored[s], i * 16 + STORE_CREDIT)
                    act.wait_ge(rstd_ready, i * 2 + s + 1)
                    for t in range(TT):
                        act.wait_ge(transposed, n + t + 1)
                        nc.scalar.activation(hi[:, t % 2], x[:, s, t], ACT.Identity, bias=shift[:, t:t + 1],
                                             scale=rstd[:, t:t + 1]).then_inc(hi_ready, 1)
                        if t >= 1:
                            evacuate(i, s, t - 1)
                    evacuate(i, s, TT - 1)

        @block.tensor
        def _(pe):
            pe.sem_inc(transposed, PART_CREDIT)
            with pe.Fori(0, B // 2) as i:
                for s in range(2):
                    n = i * (2 * TT) + s * TT
                    if outproj:
                        pe.wait_ge(o_loaded[s], i * 16 + 16)
                        for t in range(TT):
                            pe.wait_ge(y_read, n + t + 1)
                            for k, (a, c) in enumerate(PASSES):
                                for g in range(NG):
                                    last = nc.tensor.matmul(
                                        yp[:, t % 4], ot[:, s, a, g, t * P:(t + 1) * P], w_out[:, c, g, :],
                                        start=(k == 0 and g == 0), stop=(k == len(PASSES) - 1 and g == NG - 1))
                            last.then_inc(y_ready, 1)
                    for t in range(TT):
                        pe.wait_ge(lo_ready, n + t + 1 + X_CREDIT)
                        pe.wait_ge(hi_ready, n + t + 1)
                        pe.wait_ge(evacuated, n + t + 1)
                        for l, part in ((0, hi), (1, lo)):
                            for e in range(EC):
                                last = nc.tensor.transpose(tp[:, t % 4, (l * EC + e) * P:(l * EC + e + 1) * P],
                                                           part[:, t % 2, e * P:(e + 1) * P], ident16[:, :])
                        last.then_inc(transposed, 1)


UNITS = HG * EC + HG * TT
CHUNKS = HG * (EC + 2 * EC)
PROJ_TILES = 6
PROJ_STEPS = EC * 3
SCORE_BANKS, PROB_SLOTS, MAX_BANKS, GENS = 3, 4, 2, 4
CHUNKS_BY = 37
TILE_UNITS = UNITS // PROJ_TILES
STEPS_PER_UNIT = 2
MAX_T_AT = 39
LAG = 2
COPY_AT = (HG * EC - 1 + LAG, LAG - 1)
INVERT_AT = ((19, 21, 23, 25), (3, 5, 7, 9))
NORMALISE_AT = (27, 11)
NORM_STEPS = 6
STACK_DMAS = 6 * HG


def unit_block(u):
    half, r = (0, u) if u < HG * EC else (1, u - HG * EC)
    h, j = divmod(r, EC if half == 0 else TT)
    return half, h, j, max(0, j * P - half * HALF)


DIAGONAL = [u for u in range(UNITS) if unit_block(u)[2] * P >= unit_block(u)[0] * HALF]


def chunks_at(u):
    return range(min(CHUNKS, u * CHUNKS // CHUNKS_BY), min(CHUNKS, (u + 1) * CHUNKS // CHUNKS_BY))


def proj_steps_at(u):
    tile, r = divmod(u, TILE_UNITS)
    return tile, range(max(0, r - 1) * STEPS_PER_UNIT, min(PROJ_STEPS, r * STEPS_PER_UNIT))


def proj_tile_done(u):
    tile, steps = proj_steps_at(u)
    return tile if PROJ_STEPS - 1 in steps else None


def chunk_block(c):
    h, r = divmod(c, CHUNKS // HG)
    if r < EC:
        return h, r, 0, (r + 1) * P, True
    i, second = EC + (r - EC) // 2, (r - EC) % 2
    return (h, i, HALF, (i - EC + 1) * P, True) if second else (h, i, 0, HALF, False)


def attention(nc, xt_dram, o_dram, m_dram, w_qkv, exp_scale, ident16, identb, neg_m, neg_s):
    with ExitStack() as ctx:
        def sb(name, shape, dt):
            return ctx.enter_context(nc.sbuf_tensor(f"at_{name}", shape, dt))

        def ps(name, shape, dt=F32):
            return ctx.enter_context(nc.psum_tensor(f"at_{name}", shape, dt))

        def sem(name):
            return ctx.enter_context(nc.semaphore(f"at_{name}"))

        xt = sb("xt", [P, HL, EC, T], F16)
        stage = sb("stage", [P, 2, HL, T], F16)
        qs = sb("qs", [P, GENS, HG, T], F16)
        ks = sb("ks", [P, GENS, HG, T], F16)
        v = sb("v", [P, GENS, TT, P], F32)
        probs = sb("probs", [P, PROB_SLOTS, HALF], F32)
        ones = sb("ones", [P, D], F32)
        mx = sb("mx", [P, 2, HG, TT], F32)
        mxall = sb("mxall", [P, HG, TT], F32)
        m32 = sb("m32", [P, HG * TT], F32)
        mparts = sb("mparts", [P, P // (HG * TT), HG * TT], F16)
        mt = sb("mt", [2 * HG * TT, P], F16)
        o_raw = sb("o_raw", [P, HALF], F32)
        l_raw = sb("l_raw", [P, HALF], F32)
        l_inv = sb("l_inv", [P, HALF], F32)
        o_norm = sb("o_norm", [P, HALF], F32)
        o_part = sb("o_part", [P, 2, HL, HALF], F16)

        score_ps = ps("score_ps", [P, SCORE_BANKS, HALF])
        max_ps = ps("max_ps", [P, MAX_BANKS, HALF])
        proj_ps = ps("proj_ps", [P, HALF])
        out_ps = ps("out_ps", [P, HALF])
        sum_ps = ps("sum_ps", [P, HALF])

        setup = sem("setup")
        xt_loaded = [sem("xt_loaded0"), sem("xt_loaded1")]
        proj_ready, proj_read, hi_done = sem("proj_ready"), sem("proj_read"), sem("hi_done")
        stage_ready, stacked = sem("stage_ready"), sem("stacked")
        chunk_ready, chunk_read, max_stored = sem("chunk_ready"), sem("chunk_read"), sem("max_stored")
        max_step, max_ready = sem("max_step"), sem("max_ready")
        max_t_ready, max_t_copied, max_rows = sem("max_t_ready"), sem("max_t_copied"), sem("max_rows")
        scores_ready, exp_done, pv_done = sem("scores_ready"), sem("exp_done"), sem("pv_done")
        sums_ready, out_copied, l_copied = sem("sums_ready"), sem("out_copied"), sem("l_copied")
        norm_step, o_ready, o_stored = sem("norm_step"), sem("o_ready"), [sem("o_stored0"), sem("o_stored1")]
        block = ctx.enter_context(nc.Block())

        def groups(eng, body):
            body(0, 0, 0, lambda k: True)
            with eng.Fori(0, B - 1) as b:
                for g in range(1, NG):
                    body(b * NG + g, g, b, lambda k: True)
                body(b * NG + NG, 0, b + 1, lambda k: True)
            for g in range(1, NG):
                body((B - 1) * NG + g, g, B - 1, lambda k, g=g: g + k < NG)

        @block.sync
        def _(sp):
            def load_tokens(b, half):
                cols = slice(half * HALF, (half + 1) * HALF)
                sp.dma_start(xt[:, :, :, cols], xt_dram[bass.ds(b, 1), :, :, :, cols]
                             .rearrange("o p l e t -> p (o l) e t")).then_inc(xt_loaded[half], 16)

            def stack_group(gen, group):
                for which, dst, order in ((0, qs, (0, 1, 0)), (1, ks, (0, 0, 1))):
                    sp.wait_ge(proj_read, group * PROJ_TILES + 2 * which + 2 + 1)
                    for h in range(HG):
                        for r, l in enumerate(order):
                            sp.dma_start(dst[r * D:(r + 1) * D, gen, h, :], stage[h * D:(h + 1) * D, which, l, :]
                                         ).then_inc(stacked, 16)

            def max_rows_in(gen, group):
                sp.wait_ge(max_t_copied, group + 1)
                if not (isinstance(group, int) and group == 0):
                    sp.wait_ge(max_rows, group * 16)
                sp.dma_start(m_dram.rearrange("r h (i q) -> (r h i) q", q=P), mt[:, :]).then_inc(max_stored, 16)
                sp.wait_ge(max_stored, 16 * (group + 1))
                sp.dma_start(qs[3 * D:3 * D + 2, gen, :, :], m_dram).then_inc(max_rows, 16)

            def store_output(n, g, half):
                sp.wait_ge(o_ready, n * 2 + half + 1)
                sp.dma_start(o_dram[bass.ds(n, 1), :, :, half * HALF:(half + 1) * HALF]
                             .rearrange("o p l t -> p (o l) t"), o_part[:, half, :, :]).then_inc(o_stored[half], 16)

            for half in range(2):
                sp.sem_inc(o_stored[half], 16)
            load_tokens(0, 0)
            load_tokens(0, 1)
            stack_group(0, 0)
            stack_group(1, 1)
            max_rows_in(0, 0)

            def body(n, g, b, ahead):
                if not (isinstance(n, int) and n == 0):
                    store_output(n - 1, (g - 1) % NG, 1)
                if ahead(2):
                    stack_group((g + 2) % GENS, n + 2)
                store_output(n, g, 0)
                if g == 1 and ahead(3):
                    sp.wait_ge(proj_ready, (n + 2) * PROJ_TILES + PROJ_TILES - 1)
                    load_tokens(b + 1, 0)
                if ahead(1):
                    max_rows_in((g + 1) % GENS, n + 1)
                if g == 1 and ahead(3):
                    sp.wait_ge(proj_ready, (n + 2) * PROJ_TILES + PROJ_TILES)
                    load_tokens(b + 1, 1)

            groups(sp, body)
            store_output(B * NG - 1, NG - 1, 1)
            for half in range(2):
                sp.wait_ge(o_stored[half], 16 * B * NG + 16)

        @block.gpsimd
        def _(pool):
            nc.gpsimd.memset(ks[3 * D:P, :, :, :], SHIFT_ROW).then_inc(setup, 1)
            pool.wait_ge(setup, 1)
            nc.gpsimd.memset(ones[:, :], 1.0).then_inc(setup, 1)
            nc.gpsimd.memset(mx[:, :, :, :], MASKED).then_inc(setup, 1)
            nc.gpsimd.memset(mparts[:, :, :], 0.0).then_inc(setup, 1)

        @block.tensor
        def _(pe):
            pe.sem_inc(pv_done, PROB_SLOTS)

            def projection(g, tile, step, group):
                if step == 0:
                    pe.wait_ge(proj_read, group * PROJ_TILES + tile + 1)
                e, k = divmod(step, len(PASSES))
                a, c = PASSES[k]
                start, stop = step == 0, step == PROJ_STEPS - 1
                if tile < 4:
                    which, half = divmod(tile, 2)
                    last = nc.tensor.matmul(proj_ps[:, :],
                                            w_qkv[:, a, e, which * E + g * P:which * E + (g + 1) * P],
                                            xt[:, c, e, half * HALF:(half + 1) * HALF], start=start, stop=stop)
                else:
                    for i in range(EC):
                        t = (tile - 4) * EC + i
                        last = nc.tensor.matmul(proj_ps[:, i * P:(i + 1) * P], xt[:, a, e, t * P:(t + 1) * P],
                                                w_qkv[:, c, e, 2 * E + g * P:2 * E + (g + 1) * P],
                                                start=start and i == 0, stop=stop, skip_group_check=True)
                if stop:
                    last.then_inc(proj_ready, 1)

            def max_chunk(gen, c, count, group):
                h, i, k0, width, diagonal = chunk_block(c)
                if c == 0 and not (isinstance(count, int) and count == 0):
                    pe.wait_ge(max_t_copied, group)
                pe.wait_ge(chunk_read, count + 1)
                bank = max_ps[:, c % MAX_BANKS]
                last = nc.tensor.matmul(bank[:, 0:width], qs[0:3 * D, gen, h, i * P:(i + 1) * P],
                                        ks[0:3 * D, gen, h, k0:k0 + width], start=True, stop=not diagonal)
                if diagonal:
                    last = nc.tensor.matmul(bank[:, width - P:width], identb[:, :], neg_m[:, :], start=False, stop=True)
                last.then_inc(chunk_ready, 1)

            def max_transpose(group):
                pe.wait_ge(max_ready, group + 1)
                nc.tensor.transpose(max_ps[:, 0].bitcast(F16)[:, 0:P], mparts[:, :, :].rearrange("p r c -> p (r c)"),
                                    ident16[:, :]).then_inc(max_t_ready, 1)

            def scores(gen, u, count):
                _, h, j, q0 = unit_block(u)
                half = unit_block(u)[0]
                diagonal = j * P >= half * HALF
                pe.wait_ge(exp_done, count + 1)
                bank = score_ps[:, u % SCORE_BANKS]
                last = nc.tensor.matmul(bank[:, 0:HALF - q0], ks[0:3 * D + 2, gen, h, j * P:(j + 1) * P],
                                        qs[0:3 * D + 2, gen, h, half * HALF + q0:(half + 1) * HALF],
                                        start=True, stop=not diagonal)
                if diagonal:
                    last = nc.tensor.matmul(bank[:, 0:P], identb[:, :], neg_s[:, :], start=False, stop=True)
                last.then_inc(scores_ready, 1)

            def values(gen, u, count, halves):
                half, h, j, q0 = unit_block(u)
                end = EC - 1 if half == 0 else TT - 1
                pe.wait_ge(exp_done, count + 1 + SCORE_BANKS)
                if h == 0 and j == 0:
                    pe.wait_ge(out_copied, halves + 1)
                    pe.wait_ge(l_copied, halves + 1)
                pt = probs[:, u % PROB_SLOTS, 0:HALF - q0]
                rows = slice(h * D, (h + 1) * D)
                nc.tensor.matmul(out_ps[rows, q0:HALF], v[:, gen, j, rows], pt, start=(j == 0), stop=(j == end),
                                 tile_position=(0, h * D))
                last = nc.tensor.matmul(sum_ps[rows, q0:HALF], ones[:, :], pt, start=(j == 0), stop=(j == end),
                                        tile_position=(0, h * D))
                last.then_inc(pv_done, 1)

            pe.wait_ge(setup, 4)
            for half in range(2):
                pe.wait_ge(xt_loaded[half], 16)
            for tile in range(PROJ_TILES):
                for step in range(PROJ_STEPS):
                    projection(0, tile, step, 0)
            for tile in range(PROJ_TILES):
                for step in range(PROJ_STEPS):
                    projection(1, tile, step, 1)
            pe.wait_ge(stacked, 16 * STACK_DMAS)
            for c in range(CHUNKS):
                max_chunk(0, c, c, 0)
            max_transpose(0)

            def body(n, g, b, ahead):
                first = isinstance(n, int) and n == 0
                for u in range(UNITS):
                    if u == 0:
                        pe.wait_ge(max_rows, n * 16 + 16)
                    scores(g, u, n * UNITS + u)
                    if ahead(1):
                        if u == 0:
                            pe.wait_ge(stacked, n * (16 * STACK_DMAS) + 32 * STACK_DMAS)
                        for c in chunks_at(u):
                            max_chunk((g + 1) % GENS, c, (n + 1) * CHUNKS + c, n + 1)
                        if u == MAX_T_AT:
                            max_transpose(n + 1)
                    if ahead(2):
                        tile, steps = proj_steps_at(u)
                        for step in steps:
                            if g == 2 and step == 0 and tile < 2:
                                pe.wait_ge(xt_loaded[tile], b * 16 + 32)
                            projection((g + 2) % NG, tile, step, n + 2)
                    if u >= LAG:
                        past = u - LAG
                        values(g, past, n * UNITS + past, n * 2 + (0 if past < HG * EC else 1))
                    elif not first:
                        past = u - LAG + UNITS
                        values((g - 1) % GENS, past, n * UNITS - UNITS + past, n * 2 - 1)
            groups(pe, body)
            for past in range(UNITS - LAG, UNITS):
                values(NG - 1, past, (B * NG - 1) * UNITS + past, B * NG * 2 - 1)

        @block.scalar
        def _(act):
            act.sem_inc(exp_done, SCORE_BANKS)
            act.sem_inc(out_copied, 1)

            def copy_projection(gen, tile, group):
                act.wait_ge(proj_ready, group * PROJ_TILES + tile + 1)
                if tile < 4:
                    which, half = divmod(tile, 2)
                    if tile == 0 and not (isinstance(group, int) and group == 0):
                        act.wait_ge(stacked, group * (16 * STACK_DMAS))
                    nc.scalar.activation(stage[:, which, 0, half * HALF:(half + 1) * HALF], proj_ps[:, :],
                                         ACT.Copy).then_inc(hi_done, 1)
                else:
                    t0 = (tile - 4) * EC
                    nc.scalar.activation(v[:, gen, t0:t0 + EC, :], proj_ps[:, :].rearrange("p (t f) -> p t f", t=EC),
                                         ACT.Copy).then_inc(proj_read, 1)

            def copy_output(m, half):
                k = m * 2 + half
                act.wait_ge(pv_done, m * UNITS + (HG * EC if half == 0 else UNITS) + PROB_SLOTS)
                act.wait_ge(norm_step, k * NORM_STEPS + NORM_STEPS)
                nc.scalar.activation(o_raw[:, :], out_ps[:, :], ACT.Copy).then_inc(out_copied, 1)

            for group in range(2):
                for tile in range(PROJ_TILES):
                    copy_projection(group, tile, group)

            def body(n, g, b, ahead):
                for u in range(UNITS):
                    q0 = unit_block(u)[3]
                    count = n * UNITS + u
                    act.wait_ge(scores_ready, count + 1)
                    act.wait_ge(pv_done, count + 1)
                    nc.scalar.activation(probs[:, u % PROB_SLOTS, 0:HALF - q0],
                                         score_ps[:, u % SCORE_BANKS, 0:HALF - q0], ACT.Exp,
                                         scale=exp_scale[:, 0:1]).then_inc(exp_done, 1)
                    if u == COPY_AT[0]:
                        copy_output(n, 0)
                    if u == COPY_AT[1] and not (isinstance(n, int) and n == 0):
                        copy_output(n - 1, 1)
                    if ahead(2) and u >= 1 and proj_tile_done(u - 1) is not None:
                        tile = proj_tile_done(u - 1)
                        copy_projection((g + 2) % GENS, tile, n + 2)

            groups(act, body)
            copy_output(B * NG - 1, 1)

        @block.vector
        def _(dve):
            dve.sem_inc(proj_read, 1)
            dve.sem_inc(chunk_read, MAX_BANKS)
            dve.sem_inc(l_copied, 1)
            dve.sem_inc(norm_step, NORM_STEPS)
            dve.wait_ge(setup, 4)

            def low_parts(tile, group):
                which, half = divmod(tile, 2)
                cols = slice(half * HALF, (half + 1) * HALF)
                dve.wait_ge(hi_done, group * 4 + tile + 1)
                nc.vector.tensor_tensor(stage[:, which, 1, cols], proj_ps[:, :], stage[:, which, 0, cols],
                                        ALU.subtract).then_inc(proj_read, 1)

            def reduce_chunk(c, count):
                h, i, k0, width, _ = chunk_block(c)
                dve.wait_ge(chunk_ready, count + 1)
                nc.vector.tensor_reduce(mx[:, 1 if k0 else 0, h, i:i + 1], max_ps[:, c % MAX_BANKS, 0:width],
                                        AX_X, ALU.max).then_inc(chunk_read, 1)

            def prepare_max(group):
                dve.wait_ge(chunk_read, group * CHUNKS + CHUNKS + MAX_BANKS)
                nc.vector.tensor_tensor(mxall[:, :, :], mx[:, 0], mx[:, 1], ALU.max).then_inc(max_step, 1)
                dve.wait_ge(max_step, group * 3 + 1)
                nc.vector.tensor_scalar(m32[:, :], mxall[:, :, :].rearrange("p h i -> p (h i)"), -1.0 / SHIFT_ROW,
                                        None, ALU.mult).then_inc(max_step, 1)
                dve.wait_ge(max_step, group * 3 + 2)
                nc.vector.tensor_copy(mparts[:, 0], m32[:, :]).then_inc(max_step, 1)
                dve.wait_ge(max_step, group * 3 + 3)
                nc.vector.tensor_tensor(mparts[:, 1], m32[:, :], mparts[:, 0], ALU.subtract).then_inc(max_ready, 1)

            def copy_max_t(group):
                dve.wait_ge(max_t_ready, group + 1)
                if not (isinstance(group, int) and group == 0):
                    dve.wait_ge(max_rows, group * 16)
                nc.vector.tensor_copy(mt[:, :], max_ps[:, 0].bitcast(F16)[0:2 * HG * TT, 0:P]
                                      ).then_inc(max_t_copied, 1)

            def copy_sums(n, half):
                dve.wait_ge(pv_done, n * UNITS + (HG * EC if half == 0 else UNITS) + PROB_SLOTS)
                nc.vector.tensor_copy(l_raw[:, :], sum_ps[:, :]).then_inc(l_copied, 1)

            def invert(n, half, quarter):
                k = n * 2 + half
                cols = slice(quarter * P, (quarter + 1) * P)
                if quarter == 0:
                    dve.wait_ge(l_copied, k + 1 + 1)
                nc.vector.reciprocal(l_inv[:, cols], l_raw[:, cols]).then_inc(norm_step, 1)

            def normalise(n, half):
                k = n * 2 + half
                done = k * NORM_STEPS + NORM_STEPS
                dve.wait_ge(norm_step, done + 4)
                dve.wait_ge(out_copied, k + 1 + 1)
                nc.vector.tensor_tensor(o_norm[:, :], o_raw[:, :], l_inv[:, :], ALU.mult).then_inc(norm_step, 1)
                dve.wait_ge(norm_step, done + 5)
                dve.wait_ge(o_stored[half], n * 16 + 16)
                nc.vector.tensor_copy(o_part[:, half, 0], o_norm[:, :]).then_inc(norm_step, 1)
                dve.wait_ge(norm_step, done + 6)
                nc.vector.tensor_tensor(o_part[:, half, 1], o_norm[:, :], o_part[:, half, 0], ALU.subtract
                                        ).then_inc(o_ready, 1)

            for group in range(2):
                for tile in range(4):
                    low_parts(tile, group)
            for c in range(CHUNKS):
                reduce_chunk(c, c)
            prepare_max(0)
            copy_max_t(0)

            def body(n, g, b, ahead):
                for u in range(UNITS):
                    if ahead(1):
                        for c in chunks_at(u):
                            reduce_chunk(c, (n + 1) * CHUNKS + c)
                            if c == CHUNKS - 1:
                                prepare_max(n + 1)
                        if u == MAX_T_AT:
                            copy_max_t(n + 1)
                    if ahead(2) and u >= 1 and proj_tile_done(u - 1) in range(4):
                        tile = proj_tile_done(u - 1)
                        low_parts(tile, n + 2)
                    for half, m in ((0, n), (1, n - 1)):
                        if half == 1 and isinstance(n, int) and n == 0:
                            continue
                        if u == COPY_AT[half]:
                            copy_sums(m, half)
                        if u in INVERT_AT[half]:
                            invert(m, half, INVERT_AT[half].index(u))
                        if u == NORMALISE_AT[half]:
                            normalise(m, half)

            groups(dve, body)
            copy_sums(B * NG - 1, 1)
            for quarter in range(4):
                invert(B * NG - 1, 1, quarter)
            normalise(B * NG - 1, 1)


GATES = 3
STEPS = 4


def recurrence(nc, xt_dram, w_gates, u_gates, inv, bias, c_start, c_scale, c_parts):
    with ExitStack() as ctx:
        def sb(name, shape, dt):
            return ctx.enter_context(nc.sbuf_tensor(f"rc_{name}", shape, dt))

        def sem(name):
            return ctx.enter_context(nc.semaphore(f"rc_{name}"))

        xt = sb("xt", [P, 2, HL, EC, HALF], F16)
        c = sb("c", [P, 2, EC, HALF], F32)
        act_out = sb("act_out", [P, 2, GATES, HALF], F32)
        fc = sb("fc", [P, HALF], F32)
        ig = sb("ig", [P, HALF], F32)
        total = sb("total", [P, HALF], F32)
        halfscale = sb("halfscale", [P, GATES, EC], F32)
        halfbias = sb("halfbias", [P, GATES, EC], F32)
        z = ctx.enter_context(nc.psum_tensor("rc_z", [P, 2 * GATES, HALF], F32))
        x_loaded, z_ready, z_read = [sem("x_loaded0"), sem("x_loaded1")], sem("z_ready"), sem("z_read")
        own, c_ready, consts = sem("own"), sem("c_ready"), sem("consts")
        block = ctx.enter_context(nc.Block())
        ROUND = EC * STEPS
        FACTOR = (0.5, 0.5, 1.0)

        @block.sync
        def _(sp):
            with sp.Fori(0, B // 2) as i:
                for s in range(STEPS):
                    t, half = divmod(s, 2)
                    sp.wait_ge(z_ready, i * (ROUND * GATES) + (s + 1) * EC * GATES)
                    sp.dma_start(xt[:, s % 2],
                                 xt_dram[bass.ds(i * 2 + t, 1), :, :, :, half * HALF:(half + 1) * HALF]
                                 .rearrange("o p l e t -> p (o l) e t")).then_inc(x_loaded[s % 2], 16)

        @block.tensor
        def _(pe):
            pe.sem_inc(z_ready, 2 * EC * GATES)
            with pe.Fori(0, B // 2) as i:
                for s in range(STEPS):
                    t, half = divmod(s, 2)
                    pe.wait_ge(x_loaded[s % 2], i * (8 * STEPS) + 16 * (s // 2 + 1))
                    for m in range(EC):
                        k = s * EC + m
                        for gate in range(GATES):
                            bank = z[:, (k % 2) * GATES + gate]
                            pe.wait_ge(z_read, i * (ROUND * GATES) + k * GATES + gate + 1)
                            for q, (a, l) in enumerate(PASSES):
                                for e in range(EC):
                                    nc.tensor.matmul(bank, w_gates[:, a, e, gate * E + m * P:gate * E + (m + 1) * P],
                                                     xt[:, s % 2, l, e, :], start=(q == 0 and e == 0), stop=False)
                            if m == 0 and gate == 0:
                                pe.wait_ge(c_ready, i * ROUND + s * EC + EC)
                            for q, (a, l) in enumerate(PASSES):
                                for e in range(EC):
                                    last = nc.tensor.matmul(
                                        bank, u_gates[:, a, e, gate * E + m * P:gate * E + (m + 1) * P],
                                        c_parts[:, half, t, l, e, :], start=False,
                                        stop=(q == len(PASSES) - 1 and e == EC - 1))
                            last.then_inc(z_ready, 1)

        @block.scalar
        def _(act):
            act.sem_inc(z_read, 2 * GATES)
            act.wait_ge(consts, GATES * 2)
            with act.Fori(0, B // 2) as i:
                for s in range(STEPS):
                    for m in range(EC):
                        k = s * EC + m
                        act.wait_ge(c_ready, i * ROUND + k + 7)
                        for gate in range(GATES):
                            act.wait_ge(z_ready, i * (ROUND * GATES) + k * GATES + gate + 1 + 2 * EC * GATES)
                            nc.scalar.activation(act_out[:, k % 2, gate], z[:, (k % 2) * GATES + gate], ACT.Tanh,
                                                 bias=halfbias[:, gate, m:m + 1],
                                                 scale=halfscale[:, gate, m:m + 1]).then_inc(z_read, 1)

        @block.vector
        def _(dve):
            for gate in range(GATES):
                nc.vector.tensor_scalar(halfscale[:, gate], inv[:, gate], FACTOR[gate], None, ALU.mult
                                        ).then_inc(consts, 1)
                nc.vector.tensor_scalar(halfbias[:, gate], bias[:, gate], FACTOR[gate], None, ALU.mult
                                        ).then_inc(consts, 1)
            ch = Chain(dve, own)
            for half in range(2):
                for m in range(EC):
                    ch.after(nc.vector.tensor_copy(c[:, half, m], c_start[:, m:m + 1].broadcast_to([P, HALF])))
                    ch.after(nc.vector.tensor_scalar(c_parts[:, half, 0, 0, m], c[:, half, m], c_scale[:, 0:1], None,
                                                     ALU.mult))
                    nc.vector.scalar_tensor_tensor(c_parts[:, half, 0, 1, m], c[:, half, m], c_scale[:, 0:1],
                                                   c_parts[:, half, 0, 0, m], ALU.mult, ALU.subtract
                                                   ).then_inc(c_ready, 1)
            before = ch.count
            LINKS = 5
            with dve.Fori(0, B // 2) as i:
                ch = Chain(dve, own, i * (ROUND * LINKS) + before)
                for s in range(STEPS):
                    t, half = divmod(s, 2)
                    for m in range(EC):
                        k = s * EC + m
                        dve.wait_ge(z_read, i * (ROUND * GATES) + (k + 1) * GATES + 2 * GATES)
                        f, g_in, g_cell = (act_out[:, k % 2, gate] for gate in range(GATES))
                        new = c_parts[:, half, 1 - t]
                        ch.after(nc.vector.scalar_tensor_tensor(fc[:, :], f, 1.0, c[:, half, m], ALU.add, ALU.mult))
                        ch.after(nc.vector.scalar_tensor_tensor(ig[:, :], g_in, 1.0, g_cell, ALU.add, ALU.mult))
                        ch.after(nc.vector.tensor_tensor(total[:, :], fc[:, :], ig[:, :], ALU.add))
                        ch.after(nc.vector.tensor_scalar(c[:, half, m], total[:, :], 0.5, None, ALU.mult))
                        ch.after(nc.vector.tensor_scalar(new[:, 0, m], c[:, half, m], c_scale[:, 0:1], None, ALU.mult))
                        nc.vector.scalar_tensor_tensor(new[:, 1, m], c[:, half, m], c_scale[:, 0:1], new[:, 0, m],
                                                       ALU.mult, ALU.subtract).then_inc(c_ready, 1)


def output_layer(nc, xt_dram, x1, out, w_o, u_o, inv_dram, bo, c_parts):
    with ExitStack() as ctx:
        def sb(name, shape, dt):
            return ctx.enter_context(nc.sbuf_tensor(f"ol_{name}", shape, dt))

        def sem(name):
            return ctx.enter_context(nc.semaphore(f"ol_{name}"))

        def slots(name):
            return [sem(f"{name}{s}") for s in range(2)]

        xt = sb("xt", [P, 2, HL, EC, T], F16)
        res = sb("res", [P, 2, TT, E], F32)
        state = sb("state", [P, TT, E], F32)
        scaled = sb("scaled", [P, 2, E], F32)
        summed = sb("summed", [P, 2, E], F32)
        h = sb("h", [P, 2, E], F32)
        inv_row = sb("inv_row", [P, E], F32)
        bo_row = sb("bo_row", [P, E], F32)
        z = ctx.enter_context(nc.psum_tensor("ol_z", [P, 4, E], F32))
        rows, x_loaded, res_loaded = sem("rows"), slots("x_loaded"), slots("res_loaded")
        z_ready, z_read, summed_ready, h_ready = sem("z_ready"), sem("z_read"), sem("summed_ready"), sem("h_ready")
        done, stored = sem("done"), slots("stored")
        block = ctx.enter_context(nc.Block())
        BANKS = 4

        @block.sync
        def _(sp):
            sp.dma_start(inv_row[:, :], inv_dram.partition_broadcast(P)).then_inc(rows, 16)
            sp.dma_start(bo_row[:, :], bo.partition_broadcast(P)).then_inc(rows, 16)
            def load(b, s):
                sp.dma_start(xt[:, s], xt_dram[bass.ds(b, 1)].rearrange("o p l e t -> p (o l) e t")
                             ).then_inc(x_loaded[s], 16)
                sp.dma_start(res[:, s], x1[bass.ds(b, 1)].rearrange("o (t p) e -> p (o t) e", p=P)
                             ).then_inc(res_loaded[s], 16)

            def pair(i, last):
                for s in range(2):
                    if not (last and s == 1):
                        sp.wait_ge(stored[1 - s], i * 16 + (16 if s == 0 else 32))
                        load(i * 2 + s + 1, 1 - s)
                    sp.wait_ge(done, i * (2 * TT) + (s + 1) * TT)
                    sp.dma_start(out[bass.ds(i * 2 + s, 1)].rearrange("o (t p) e -> p (o t) e", p=P), res[:, s]
                                 ).then_inc(stored[s], 16)

            for s in range(2):
                sp.sem_inc(stored[s], 16)
            load(0, 0)
            with sp.Fori(0, B // 2 - 1) as i:
                pair(i, False)
            pair(B // 2 - 1, True)
            for s in range(2):
                sp.wait_ge(stored[s], 16 * (B // 2) + 16)

        @block.tensor
        def _(pe):
            for n in range(TT):
                half, col = divmod(n, EC)
                if n >= BANKS:
                    pe.wait_ge(z_read, n - BANKS + 1)
                for q, (a, l) in enumerate(PASSES):
                    for e in range(EC):
                        last = nc.tensor.matmul(z[:, n % BANKS], c_parts[:, half, 0, a, e, col * P:(col + 1) * P],
                                                u_o[:, l, e, :], start=(q == 0 and e == 0),
                                                stop=(q == len(PASSES) - 1 and e == EC - 1))
                last.then_inc(z_ready, 1)
            with pe.Fori(0, B // 2) as i:
                for s in range(2):
                    pe.wait_ge(x_loaded[s], i * 16 + 16)
                    for t in range(TT):
                        n = i * (2 * TT) + s * TT + t + TT
                        pe.wait_ge(z_read, n - BANKS + 1)
                        for q, (a, l) in enumerate(PASSES):
                            for e in range(EC):
                                last = nc.tensor.matmul(z[:, t % BANKS], xt[:, s, a, e, t * P:(t + 1) * P],
                                                        w_o[:, l, e, :], start=(q == 0 and e == 0),
                                                        stop=(q == len(PASSES) - 1 and e == EC - 1))
                        last.then_inc(z_ready, 1)

        @block.scalar
        def _(act):
            with act.Fori(0, B // 2) as i:
                for s in range(2):
                    for t in range(TT):
                        n = i * (2 * TT) + s * TT + t
                        act.wait_ge(summed_ready, n + TT + 1)
                        nc.scalar.activation(h[:, t % 2], summed[:, t % 2], ACT.Tanh).then_inc(h_ready, 1)

        @block.vector
        def _(dve):
            dve.wait_ge(rows, 32)
            for n in range(TT):
                dve.wait_ge(z_ready, n + 1)
                nc.vector.tensor_tensor(scaled[:, n % 2], z[:, n % BANKS], inv_row[:, :], ALU.mult).then_inc(z_read, 1)
                dve.wait_ge(z_read, n + 1)
                nc.vector.tensor_tensor(state[:, n], scaled[:, n % 2], bo_row[:, :], ALU.add).then_inc(summed_ready, 1)
            dve.wait_ge(summed_ready, TT)
            with dve.Fori(0, B // 2) as i:
                for s in range(2):
                    dve.wait_ge(res_loaded[s], i * 16 + 16)

                    def residual(i, s, t):
                        n = i * (2 * TT) + s * TT + t
                        dve.wait_ge(h_ready, n + 1)
                        nc.vector.tensor_tensor(res[:, s, t], res[:, s, t], h[:, t % 2], ALU.add).then_inc(done, 1)

                    for t in range(TT):
                        n = i * (2 * TT) + s * TT + t + TT
                        dve.wait_ge(z_ready, n + 1)
                        nc.vector.tensor_tensor(scaled[:, t % 2], z[:, t % BANKS], inv_row[:, :], ALU.mult
                                                ).then_inc(z_read, 1)
                        dve.wait_ge(z_read, n + 1)
                        if t >= 2:
                            residual(i, s, t - 2)
                        nc.vector.tensor_tensor(summed[:, t % 2], scaled[:, t % 2], state[:, t], ALU.add
                                                ).then_inc(summed_ready, 1)
                    residual(i, s, TT - 2)
                    residual(i, s, TT - 1)


def build(nc, x, w_in, w_out, wf, uf, bf, wi, ui, bi, wc, uc, bc, wo, uo, bo, in_c, out):
    def scratch(name, shape, dt):
        return nc.dram_tensor(name, shape, dt, kind="Internal").ap()

    xt1 = scratch("xt1", (B, P, HL, EC, T), F16)
    xt2 = scratch("xt2", (B, P, HL, EC, T), F16)
    ot = scratch("ot", (B * NG, P, HL, T), F16)
    x1 = scratch("x1", (B, T, E), F32)
    m_dram = scratch("m_dram", (2, HG, T), F16)
    v_row = scratch("v_row", (E,), F32)
    out_row = scratch("out_row", (E,), F32)
    o_row = scratch("o_row", (E,), F32)
    with ExitStack() as ctx:
        ctx.enter_context(nc.allow_non_contiguous_dma(reason="a few vectors of 512 numbers, spread over the partitions"))

        def sb(name, shape, dt, c=ctx):
            return c.enter_context(nc.sbuf_tensor(name, shape, dt))

        ident16 = sb("ident16", [P, P], F16)
        identb = sb("identb", [P, P], BF16)
        neg_m = sb("neg_m", [P, P], BF16)
        neg_s = sb("neg_s", [P, P], BF16)
        bias = sb("bias", [P, GATES, EC], F32)
        c_start = sb("c_start", [P, EC], F32)
        c_row = sb("c_row", [P, E], F32)
        c_top = sb("c_top", [P, 1], F32)
        c_inv = sb("c_inv", [P, 1], F32)
        c_scale = sb("c_scale", [P, 1], F32)
        exp_scale = sb("exp_scale", [P, 1], F32)

        with nc.semaphore("made") as made, nc.semaphore("consts_in") as consts_in, nc.semaphore("c_steps") as c_steps, \
                nc.Block() as block:
            @block.sync
            def _(sp):
                for g, v in enumerate((bf, bi, bc)):
                    sp.dma_start(bias[:, g, :], v.rearrange("(t p) -> p t", p=P)).then_inc(consts_in, 16)
                sp.dma_start(c_start[:, :], in_c.rearrange("(t p) -> p t", p=P)).then_inc(consts_in, 16)
                sp.dma_start(c_row[:, :], in_c.partition_broadcast(P)).then_inc(consts_in, 16)

            @block.gpsimd
            def _(pool):
                for tile, value in ((ident16, 0.0), (identb, 0.0), (neg_m, 0.0), (neg_s, 0.0)):
                    nc.gpsimd.memset(tile[:, :], value).then_inc(made, 1)
                pool.wait_ge(made, 4)
                for tile in (ident16, identb):
                    nc.gpsimd.affine_select(out=tile[:, :], in_=tile[:, :], compare_op=ALU.not_equal, fill=1.0, base=0,
                                            pattern=[[-1, P]], channel_multiplier=1)
                nc.gpsimd.affine_select(out=neg_m[:, :], in_=neg_m[:, :], compare_op=ALU.is_ge, fill=MASKED, base=0,
                                        pattern=[[-1, P]], channel_multiplier=1)
                nc.gpsimd.affine_select(out=neg_s[:, :], in_=neg_s[:, :], compare_op=ALU.is_ge, fill=MASKED, base=0,
                                        pattern=[[1, P]], channel_multiplier=-1).then_inc(made, 1)
                pool.wait_ge(made, 5)

            @block.vector
            def _(dve):
                ch = Chain(dve, c_steps)
                dve.wait_ge(consts_in, 80)
                ch.after(nc.vector.tensor_reduce(c_top[:, :], c_row[:, :], AX_X, ALU.max, apply_absolute_value=True))
                ch.after(nc.vector.tensor_scalar(c_inv[:, :], c_top[:, :], 1.0, None, ALU.max))
                ch.after(nc.vector.tensor_scalar(c_inv[:, :].bitcast(U32), c_inv[:, :].bitcast(U32), EXPONENT, None,
                                                 ALU.bitwise_and))
                ch.after(nc.vector.reciprocal(c_scale[:, :], c_inv[:, :]))

        with ExitStack() as first:
            w_qkv = sb("w_qkv", [P, HL, EC, 3 * E], F16, first)
            w_o1 = sb("w_o1", [P, HL, EC, E], F16, first)
            inv1 = sb("inv1", [P, 4, EC], F32, first)
            prepare_weights(nc, "pa", [[(w_in[2 * E:3 * E], w_qkv, 2 * E)], [(w_in[0:E], w_qkv, 0)],
                                       [(w_in[E:2 * E], w_qkv, E)], [(w_out, w_o1, 0)]],
                            inv1, ident16, (1, 2), scratch_v=(0, v_row))
            with nc.semaphore("row_out") as row_out, nc.semaphore("scale_set") as scale_set, nc.Block() as block:
                @block.sync
                def _(sp):
                    sp.dma_start(out_row.rearrange("(t p) -> p t", p=P), inv1[:, 3, :]).then_inc(row_out, 16)
                    sp.wait_ge(row_out, 16)

                @block.vector
                def _(dve):
                    nc.vector.scalar_tensor_tensor(exp_scale[:, :], inv1[:, 1, 0:1], D ** -0.5, inv1[:, 2, 0:1],
                                                   ALU.mult, ALU.mult).then_inc(scale_set, 1)
                    dve.wait_ge(scale_set, 1)
            normalise_tokens(nc, "n1", x, xt1, ident16)
            attention(nc, xt1, ot, m_dram, w_qkv, exp_scale, ident16, identb, neg_m, neg_s)
            normalise_tokens(nc, "n2", x, xt2, ident16, outproj=(ot, w_o1, out_row, x1))

        w_gates = sb("w_gates", [P, HL, EC, GATES * E], F16)
        u_gates = sb("u_gates", [P, HL, EC, GATES * E], F16)
        w_o = sb("w_o", [P, HL, EC, E], F16)
        u_o = sb("u_o", [P, HL, EC, E], F16)
        inv2 = sb("inv2", [P, 4, EC], F32)
        c_parts = sb("c_parts", [P, 2, 2, HL, EC, HALF], F16)
        prepare_weights(nc, "pb", [[(w, w_gates, g * E), (u, u_gates, g * E)]
                                   for g, (w, u) in enumerate(((wf, uf), (wi, ui), (wc, uc)))] +
                        [[(wo, w_o, 0), (uo, u_o, 0)]], inv2, ident16, (), c_scale=c_inv)
        with nc.semaphore("row_out2") as row_out2, nc.Block() as block:
            @block.sync
            def _(sp):
                sp.dma_start(o_row.rearrange("(t p) -> p t", p=P), inv2[:, 3, :]).then_inc(row_out2, 16)
                sp.wait_ge(row_out2, 16)
        recurrence(nc, xt2, w_gates, u_gates, inv2, bias, c_start, c_scale, c_parts)
        output_layer(nc, xt2, x1, out, w_o, u_o, o_row, bo, c_parts)


INS = ("L0_attn_query", "L0_attn_in_proj_weight", "L0_attn_out_proj_weight", "L0_ffn_wf", "L0_ffn_uf", "L0_ffn_bf",
       "L0_ffn_wi", "L0_ffn_ui", "L0_ffn_bi", "L0_ffn_wc", "L0_ffn_uc", "L0_ffn_bc", "L0_ffn_wo", "L0_ffn_uo",
       "L0_ffn_bo", "L0_ffn_in_c")


def kernel(**inputs):
    import numpy as _np
    import concourse.bacc as _bacc
    from concourse import mybir as _mybir
    from concourse.bass_utils import run_bass_kernel_spmd as _run

    nc = _bacc.Bacc("TRN2", target_bir_lowering=False, num_devices=1)
    arrays, args = {}, []
    for name in INS:
        a = _np.ascontiguousarray(inputs[name])
        arrays[f"in_{name}"] = a
        args.append(nc.dram_tensor(f"in_{name}", a.shape, _mybir.dt.from_np(a.dtype), kind="ExternalInput").ap())
    args.append(nc.dram_tensor("out_0", (B, T, E), F32, kind="ExternalOutput").ap())
    nc.disable_value_cache = True
    build(nc, *args)
    r = _run(nc, [arrays], core_ids=[0])
    return r.results[0]["out_0"]
```

```python
from contextlib import ExitStack

import concourse.bass as bass
from concourse import mybir

ALU = mybir.AluOpType
ACT = mybir.ActivationFunctionType
AX_X = mybir.AxisListType.X
F32 = mybir.dt.float32
F16 = mybir.dt.float16
BF16 = mybir.dt.bfloat16
U32 = mybir.dt.uint32
POOL_MAX = bass.bass_isa.ReduceOp.max

P = 128
B, T, E = 8, 1024, 512
H, D = 16, 32
TT = T // P
EC = E // P
HG = P // D
NG = H // HG
HALF = T // 2
LN_EPS = 1e-5
HL = 2
EXPONENT = 0x7F800000
W_TOP = 4.0
SHIFT_ROW = 32768.0
MASKED = -3.0e38
PASSES = ((0, 0), (0, 1), (1, 0))


class Chain:

    def __init__(self, eng, sem, base=0):
        self.eng, self.sem, self.base, self.count = eng, sem, base, 0

    def after(self, instruction):
        instruction.then_inc(self.sem, 1)
        self.count += 1
        self.eng.wait_ge(self.sem, self.base + self.count)


def prepare_weights(nc, tag, jobs, inv, ident16, global_rows, scratch_v=None, c_scale=None):
    J = len(jobs)
    M = max(len(j) for j in jobs)
    with ExitStack() as ctx:
        def sb(name, shape, dt):
            return ctx.enter_context(nc.sbuf_tensor(f"{tag}_{name}", shape, dt))

        def sem(name):
            return ctx.enter_context(nc.semaphore(f"{tag}_{name}"))

        nat = sb("nat", [P, 2, M * EC, E], F32)
        part = sb("part", [P, 2, HL, M * EC, E], F16)
        rowmax = sb("rowmax", [P, M * EC], F32)
        pairmax = sb("pairmax", [P, EC], F32)
        onemax = sb("onemax", [P, 1], F32)
        allmax = sb("allmax", [P, 1], F32)
        scale = sb("scale", [P, EC], F32)
        vrow = sb("vrow", [P, E], F32)
        tp = ctx.enter_context(nc.psum_tensor(f"{tag}_tp", [P, 4, HL * EC * P], F16))
        loaded, nat_used = [sem("loaded0"), sem("loaded1")], sem("nat_used")
        transposed, evacuated, own = sem("transposed"), sem("evacuated"), sem("own")
        max_in, max_out = sem("max_in"), sem("max_out")
        vinv_ready, vinv_stored, vinv_loaded = sem("vinv_ready"), sem("vinv_stored"), sem("vinv_loaded")
        block = ctx.enter_context(nc.Block())

        loads_until = [16 * sum(len(other) for other in jobs[j % 2:j + 1:2]) for j in range(J)]
        tiles_until = [0]
        for job in jobs:
            tiles_until.append(tiles_until[-1] + len(job) * EC)

        @block.sync
        def _(sp):
            for j, job in enumerate(jobs):
                if j >= 2:
                    sp.wait_ge(nat_used, j - 1)
                for m, (w, _, _) in enumerate(job):
                    sp.dma_start(nat[:, j % 2, m * EC:(m + 1) * EC, :],
                                 w.rearrange("(t p) e -> p t e", p=P)).then_inc(loaded[j % 2], 16)
            if scratch_v is not None:
                v_job, row = scratch_v
                sp.wait_ge(vinv_ready, 1)
                sp.dma_start(row.rearrange("(t p) -> p t", p=P), inv[:, v_job, :]).then_inc(vinv_stored, 16)
                sp.wait_ge(vinv_stored, 16)
                sp.dma_start(vrow[:, :], row.partition_broadcast(P)).then_inc(vinv_loaded, 16)

        @block.gpsimd
        def _(pool):
            for k in range(len(global_rows)):
                pool.wait_ge(max_in, k + 1)
                nc.gpsimd.partition_all_reduce(allmax[:, :], onemax[:, :], P, POOL_MAX).then_inc(max_out, 1)

        @block.vector
        def _(dve):
            ch = Chain(dve, own)
            n_global = 0
            for j, job in enumerate(jobs):
                m = len(job)
                w = nat[:, j % 2]
                dve.wait_ge(loaded[j % 2], loads_until[j])
                if scratch_v is not None and j == J - 1:
                    dve.wait_ge(vinv_loaded, 16)
                    ch.after(nc.vector.tensor_tensor(w[:, 0:EC, :], w[:, 0:EC, :],
                                                     vrow[:, :].unsqueeze(1).broadcast_to([P, EC, E]), ALU.mult))
                if c_scale is not None and m == 2:
                    ch.after(nc.vector.tensor_scalar(w[:, EC:2 * EC, :], w[:, EC:2 * EC, :],
                                                     c_scale[:, 0:1], None, ALU.mult))
                ch.after(nc.vector.tensor_reduce(rowmax[:, 0:m * EC], w[:, 0:m * EC, :], AX_X, ALU.max,
                                                 apply_absolute_value=True))
                top = rowmax[:, 0:EC]
                if m == 2:
                    ch.after(nc.vector.tensor_tensor(pairmax[:, :], rowmax[:, 0:EC], rowmax[:, EC:2 * EC], ALU.max))
                    top = pairmax[:, :]
                if j in global_rows:
                    ch.after(nc.vector.tensor_reduce(onemax[:, :], top, AX_X, ALU.max))
                    n_global += 1
                    nc.vector.engine_nop().then_inc(max_in, 1)
                    dve.wait_ge(max_out, n_global)
                    top = allmax[:, 0:1].broadcast_to([P, EC])
                ch.after(nc.vector.tensor_scalar(scale[:, :], top, 1e-15, None, ALU.max))
                ch.after(nc.vector.tensor_scalar(scale[:, :].bitcast(U32), scale[:, :].bitcast(U32),
                                                 EXPONENT, None, ALU.bitwise_and))
                ch.after(nc.vector.tensor_scalar(inv[:, j, :], scale[:, :], 1.0 / W_TOP, None, ALU.mult))
                if scratch_v is not None and j == scratch_v[0]:
                    nc.vector.engine_nop().then_inc(vinv_ready, 1)
                ch.after(nc.vector.reciprocal(scale[:, :], inv[:, j, :]))
                if j >= 2:
                    dve.wait_ge(transposed, tiles_until[j - 1])
                for k in range(m):
                    ws = w[:, k * EC:(k + 1) * EC, :]
                    ch.after(nc.vector.tensor_tensor(ws, ws, scale[:, :].unsqueeze(2).broadcast_to([P, EC, E]),
                                                     ALU.mult))
                    hi = part[:, j % 2, 0, k * EC:(k + 1) * EC, :]
                    lo = part[:, j % 2, 1, k * EC:(k + 1) * EC, :]
                    ch.after(nc.vector.tensor_copy(hi, ws))
                    last = nc.vector.tensor_tensor(lo, ws, hi, ALU.subtract)
                    if k == m - 1:
                        last.then_inc(nat_used, 1)
                    else:
                        ch.after(last)

        @block.tensor
        def _(pe):
            n = 0
            for j, job in enumerate(jobs):
                pe.wait_ge(nat_used, j + 1)
                for k in range(len(job) * EC):
                    if n >= 4:
                        pe.wait_ge(evacuated, n - 3)
                    for hl in range(HL):
                        for e in range(EC):
                            last = nc.tensor.transpose(tp[:, n % 4, (hl * EC + e) * P:(hl * EC + e + 1) * P],
                                                       part[:, j % 2, hl, k, e * P:(e + 1) * P], ident16[:, :])
                    last.then_inc(transposed, 1)
                    n += 1

        @block.scalar
        def _(act):
            n = 0
            for job in jobs:
                for _, target, col in job:
                    for t in range(EC):
                        act.wait_ge(transposed, n + 1)
                        nc.scalar.activation(
                            target[:, :, :, col + t * P:col + (t + 1) * P],
                            tp[:, n % 4, :].rearrange("p (l e f) -> p l e f", l=HL, e=EC),
                            ACT.Copy).then_inc(evacuated, 1)
                        n += 1


BT = 4
BATCHES = B * TT // BT
BEHIND = 2
PART_SLOTS = 4


def batches(eng, body):
    def edge(k):
        body(0, k, lambda j: 0 <= k + j < BATCHES)

    for k in range(2):
        edge(k)
    with eng.Fori(0, (BATCHES - 4) // 4) as i:
        for s in range(2, 6):
            body(i, s, lambda j: True)
    for k in range(BATCHES - 2, BATCHES + 2):
        edge(k)


def rounds(i, s, slots):
    return i * (4 // slots) + s // slots


def normalise_tokens(nc, tag, src, dst_t, ident16, outproj=None):
    with ExitStack() as ctx:
        def sb(name, shape, dt):
            return ctx.enter_context(nc.sbuf_tensor(f"{tag}_{name}", shape, dt))

        def sem(name):
            return ctx.enter_context(nc.semaphore(f"{tag}_{name}"))

        def slots(name, count):
            return [sem(f"{name}{s}") for s in range(count)]

        x = sb("x", [P, 4, BT, E], F32)
        xh = sb("xh", [P, 2, E], F32)
        hi = sb("hi", [P, PART_SLOTS, E], F16)
        lo = sb("lo", [P, PART_SLOTS, E], F16)
        stats = sb("stats", [P, BT, 6], F32)
        mean2, diff, dev = (sb(name, [P, BT], F32) for name in ("mean2", "diff", "dev"))
        diff2, dev_all = (sb(name, [P, BT], F32) for name in ("diff2", "dev_all"))
        var = sb("var", [P, BT], F32)
        std = sb("std", [P, BT], F32)
        rstd = sb("rstd", [P, BT], F32)
        shift = sb("shift", [P, BT], F32)
        xt = sb("xt", [P, 2, HL, EC, BT * P], F16)
        tp = ctx.enter_context(nc.psum_tensor(f"{tag}_tp", [P, 4, HL * EC * P], F16))
        loaded, lo_ready, xh_ready = slots("loaded", 4), sem("lo_ready"), sem("xh_ready")
        stats_ready, moment, var_ready = sem("stats_ready"), sem("moment"), sem("var_ready")
        std_ready, inverse_ready, rstd_ready = sem("std_ready"), sem("inverse_ready"), sem("rstd_ready")
        hi_ready, transposed, evacuated, stored = sem("hi_ready"), sem("transposed"), sem("evacuated"), slots("stored", 2)
        if outproj:
            o_parts, w_out, inv_out, x1 = outproj
            ot = sb("ot", [P, 2, HL, NG, BT * P], F16)
            y = sb("y", [P, 2, E], F32)
            inv_row = sb("inv_row", [P, E], F32)
            yp = ctx.enter_context(nc.psum_tensor(f"{tag}_yp", [P, 4, E], F32))
            o_loaded, y_ready, y_read = slots("o_loaded", 2), sem("y_ready"), sem("y_read")
            x1_ready, x1_stored, row_loaded = sem("x1_ready"), slots("x1_stored", 4), sem("row_loaded")
        block = ctx.enter_context(nc.Block())
        TP_CREDIT, PART_CREDIT, Y_CREDIT, STORE_CREDIT = 4, PART_SLOTS, 4, 16

        def tokens(dram, i, s):
            half = s % 2 * BT * P
            return dram[bass.ds(i * 2 + s // 2, 1), half:half + BT * P, :].rearrange("o (t p) e -> p (o t) e", p=P)

        @block.sync
        def _(sp):
            def load(i, s):
                sp.dma_start(x[:, s % 4], tokens(src, i, s)).then_inc(loaded[s % 4], 16)

            def load_outputs(i, s):
                half = s % 2 * BT * P
                sp.dma_start(ot[:, s % 2], o_parts[bass.ds((i * 2 + s // 2) * NG, NG), :, :, half:half + BT * P]
                             .rearrange("g p l t -> p l g t")).then_inc(o_loaded[s % 2], 16)

            for s in range(2):
                sp.sem_inc(stored[s], STORE_CREDIT)
            if outproj:
                sp.dma_start(inv_row[:, :], inv_out.partition_broadcast(P)).then_inc(row_loaded, 16)
            for s in range(2):
                load(0, s)
                if outproj:
                    load_outputs(0, s)

            def body(i, s, there):
                if there(2):
                    if there(-2):
                        sp.wait_ge(lo_ready, i * (4 * BT) + (s - 1) * BT)
                        if outproj:
                            sp.wait_ge(x1_stored[(s + 2) % 4], 16 * rounds(i, s + 2, 4))
                    load(i, s + 2)
                if there(-2):
                    sp.wait_ge(evacuated, i * (4 * BT) + (s - 1) * BT + TP_CREDIT)
                    half = s % 2 * BT * P
                    sp.dma_start(dst_t[bass.ds(i * 2 + (s - 2) // 2, 1), :, :, :, half:half + BT * P]
                                 .rearrange("o p l e t -> p (o l) e t"), xt[:, s % 2]).then_inc(stored[s % 2], 16)
                if outproj and there(0):
                    sp.wait_ge(x1_ready, i * (4 * BT) + (s + 1) * BT)
                    sp.dma_start(tokens(x1, i, s), x[:, s % 4]).then_inc(x1_stored[s % 4], 16)
                    if there(2):
                        sp.wait_ge(y_ready, i * (4 * BT) + (s + 1) * BT)
                        load_outputs(i, s + 2)

            batches(sp, body)
            for s in range(2):
                sp.wait_ge(stored[s], 16 * (BATCHES // 2) + STORE_CREDIT)
            if outproj:
                for s in range(4):
                    sp.wait_ge(x1_stored[s], 16 * (BATCHES // 4))

        @block.vector
        def _(dve):
            if outproj:
                dve.sem_inc(y_read, Y_CREDIT)
                dve.wait_ge(row_loaded, 16)

            def statistics(i, s, t):
                m = i * (4 * BT) + (s * BT + t)
                if outproj:
                    dve.wait_ge(y_ready, m + 1)
                    nc.vector.tensor_tensor(y[:, t % 2], yp[:, t % 4], inv_row[:, :], ALU.mult).then_inc(y_read, 1)
                    dve.wait_ge(y_read, m + 1 + Y_CREDIT)
                    nc.vector.tensor_tensor(x[:, s % 4, t], x[:, s % 4, t], y[:, t % 2], ALU.add
                                            ).then_inc(x1_ready, 1)
                    dve.wait_ge(x1_ready, m + 1)
                nc.vector.bn_stats(stats[:, t], x[:, s % 4, t]).then_inc(stats_ready, 1)

            def variance(i, s):
                step = i * 20 + s * 5
                dve.wait_ge(stats_ready, i * (4 * BT) + (s + 1) * BT)
                nc.vector.tensor_tensor(mean2[:, :], stats[:, :, 1], stats[:, :, 4], ALU.add).then_inc(moment, 1)
                nc.vector.tensor_tensor(diff[:, :], stats[:, :, 1], stats[:, :, 4], ALU.subtract).then_inc(moment, 1)
                nc.vector.tensor_tensor(dev[:, :], stats[:, :, 2], stats[:, :, 5], ALU.add).then_inc(moment, 1)
                dve.wait_ge(moment, step + 3)
                nc.vector.tensor_tensor(diff2[:, :], diff[:, :], diff[:, :], ALU.mult).then_inc(moment, 1)
                dve.wait_ge(moment, step + 4)
                nc.vector.scalar_tensor_tensor(dev_all[:, :], diff2[:, :], E / 4.0, dev[:, :], ALU.mult, ALU.add
                                               ).then_inc(moment, 1)
                dve.wait_ge(moment, step + 5)
                nc.vector.tensor_scalar(var[:, :], dev_all[:, :], 1.0 / E, LN_EPS, ALU.mult, ALU.add
                                        ).then_inc(var_ready, 1)

            def scale_and_shift(i, s):
                dve.wait_ge(std_ready, i * 4 + s + 1)
                nc.vector.reciprocal(rstd[:, :], std[:, :]).then_inc(inverse_ready, 1)
                dve.wait_ge(inverse_ready, i * 4 + s + 1)
                nc.vector.scalar_tensor_tensor(shift[:, :], mean2[:, :], -0.5, rstd[:, :],
                                               ALU.mult, ALU.mult).then_inc(rstd_ready, 1)
                dve.wait_ge(rstd_ready, i * 4 + s + 1)

            def normalise(i, s, t):
                m = i * (4 * BT) + (s * BT + t)
                nc.vector.tensor_scalar(xh[:, t % 2], x[:, s % 4, t], rstd[:, t:t + 1], shift[:, t:t + 1],
                                        ALU.mult, ALU.add).then_inc(xh_ready, 1)
                dve.wait_ge(xh_ready, m + 1)
                dve.wait_ge(hi_ready, m + 1)
                nc.vector.tensor_tensor(lo[:, t % PART_SLOTS], xh[:, t % 2], hi[:, t % PART_SLOTS], ALU.subtract
                                        ).then_inc(lo_ready, 1)

            def body(i, s, there):
                if there(0):
                    dve.wait_ge(loaded[s % 4], 16 * rounds(i, s, 4) + 16)
                for t in range(BT):
                    if there(0):
                        statistics(i, s, t)
                    if there(-1):
                        if t == 0:
                            scale_and_shift(i, s - 1)
                        normalise(i, s - 1, t)
                if there(0):
                    variance(i, s)

            batches(dve, body)

        @block.scalar
        def _(act):
            act.sem_inc(evacuated, TP_CREDIT)

            def evacuate(i, s, t):
                if t == 0:
                    act.wait_ge(stored[s % 2], 16 * rounds(i, s, 2) + STORE_CREDIT)
                act.wait_ge(transposed, i * (4 * BT) + (s * BT + t) + 1 + PART_CREDIT)
                nc.scalar.activation(xt[:, s % 2, :, :, t * P:(t + 1) * P],
                                     tp[:, t % 4, :].rearrange("p (l e f) -> p l e f", l=HL, e=EC),
                                     ACT.Copy).then_inc(evacuated, 1)

            def high_part(i, s, t):
                m = i * (4 * BT) + (s * BT + t)
                if t == 0:
                    act.wait_ge(rstd_ready, i * 4 + s + 1)
                act.wait_ge(transposed, m + 1)
                nc.scalar.activation(hi[:, t % PART_SLOTS], x[:, s % 4, t], ACT.Identity, bias=shift[:, t:t + 1],
                                     scale=rstd[:, t:t + 1]).then_inc(hi_ready, 1)

            def body(i, s, there):
                for t in range(BT):
                    if there(-1):
                        high_part(i, s - 1, t)
                    before, tile = divmod(t - BEHIND, BT)
                    if there(before - 1):
                        evacuate(i, s + before - 1, tile)
                if there(0):
                    act.wait_ge(var_ready, i * 4 + s + 1)
                    nc.scalar.activation(std[:, :], var[:, :], ACT.Sqrt).then_inc(std_ready, 1)

            batches(act, body)

        @block.tensor
        def _(pe):
            pe.sem_inc(transposed, PART_CREDIT)

            def project(i, s, t):
                if t == 0:
                    pe.wait_ge(o_loaded[s % 2], 16 * rounds(i, s, 2) + 16)
                pe.wait_ge(y_read, i * (4 * BT) + (s * BT + t) + 1)
                for k, (a, c) in enumerate(PASSES):
                    for g in range(NG):
                        last = nc.tensor.matmul(yp[:, t % 4], ot[:, s % 2, a, g, t * P:(t + 1) * P], w_out[:, c, g, :],
                                                start=(k == 0 and g == 0), stop=(k == len(PASSES) - 1 and g == NG - 1))
                last.then_inc(y_ready, 1)

            def transpose(i, s, t):
                m = i * (4 * BT) + (s * BT + t)
                pe.wait_ge(lo_ready, m + 1)
                pe.wait_ge(hi_ready, m + 1)
                pe.wait_ge(evacuated, m + 1)
                for l, part in ((0, hi), (1, lo)):
                    for e in range(EC):
                        last = nc.tensor.transpose(tp[:, t % 4, (l * EC + e) * P:(l * EC + e + 1) * P],
                                                   part[:, t % PART_SLOTS, e * P:(e + 1) * P], ident16[:, :])
                last.then_inc(transposed, 1)

            def body(i, s, there):
                for t in range(BT):
                    if outproj and there(0):
                        project(i, s, t)
                    before, tile = divmod(t - BEHIND, BT)
                    if there(before - 1):
                        transpose(i, s + before - 1, tile)

            batches(pe, body)


UNITS = HG * EC + HG * TT
CHUNKS = HG * (EC + 2 * EC)
PROJ_TILES = 6
PROJ_STEPS = EC * 3
SCORE_BANKS, PROB_SLOTS, MAX_BANKS, GENS = 3, 4, 2, 4
CHUNKS_BY = 36
TILE_UNITS = UNITS // PROJ_TILES
STEPS_PER_UNIT = 2
MAX_T_AT = 37
LAG = 2
COPY_AT = (HG * EC - 1 + LAG, LAG - 1)
INVERT_AT = ((36, 38, 40, 42), (3, 5, 7, 9))
NORMALISE_AT = ((43, 44, 45), (10, 11, 12))
NORM_STEPS = 6
STACK_DMAS = 6 * HG


def unit_block(u):
    half, r = (0, u) if u < HG * EC else (1, u - HG * EC)
    h, j = divmod(r, EC if half == 0 else TT)
    return half, h, j, max(0, j * P - half * HALF)


DIAGONAL = [u for u in range(UNITS) if unit_block(u)[2] * P >= unit_block(u)[0] * HALF]


def proj_steps_at(u):
    tile, r = divmod(u, TILE_UNITS)
    return tile, range(max(0, r - 1) * STEPS_PER_UNIT, min(PROJ_STEPS, r * STEPS_PER_UNIT))


def proj_tile_done(u):
    tile, steps = proj_steps_at(u)
    return tile if PROJ_STEPS - 1 in steps else None


def chunk_block(c):
    h, r = divmod(c, CHUNKS // HG)
    if r < EC:
        return h, r, 0, (r + 1) * P, True
    i, second = EC + (r - EC) // 2, (r - EC) % 2
    return (h, i, HALF, (i - EC + 1) * P, True) if second else (h, i, 0, HALF, False)


def vector_columns(u):
    columns = 0
    if u >= 1 and proj_tile_done(u - 1) in range(4):
        columns += HALF
    for half in range(2):
        if u == COPY_AT[half] or u in NORMALISE_AT[half]:
            columns += HALF
        if u in INVERT_AT[half]:
            columns += 6 * P
    return columns


def spread_chunks():
    costs = [chunk_block(c)[3] + P // 2 for c in range(CHUNKS)]
    extra = [vector_columns(u) for u in range(CHUNKS_BY)]
    rate = (sum(costs) + sum(extra)) / CHUNKS_BY
    plan, c, spent = [], 0, 0
    for u in range(CHUNKS_BY):
        spent += extra[u]
        first = c
        while c < CHUNKS and (u == CHUNKS_BY - 1 or spent + costs[c] / 2 <= rate * (u + 1)):
            spent += costs[c]
            c += 1
        plan.append(range(first, c))
    return plan + [range(0)] * (UNITS - CHUNKS_BY)


CHUNKS_AT = spread_chunks()


def attention(nc, xt_dram, o_dram, m_dram, w_qkv, exp_scale, ident16, identb, neg_m, neg_s):
    with ExitStack() as ctx:
        def sb(name, shape, dt):
            return ctx.enter_context(nc.sbuf_tensor(f"at_{name}", shape, dt))

        def ps(name, shape, dt=F32):
            return ctx.enter_context(nc.psum_tensor(f"at_{name}", shape, dt))

        def sem(name):
            return ctx.enter_context(nc.semaphore(f"at_{name}"))

        xt = sb("xt", [P, HL, EC, T], F16)
        stage = sb("stage", [P, 2, HL, T], F16)
        qs = sb("qs", [P, GENS, HG, T], F16)
        ks = sb("ks", [P, GENS, HG, T], F16)
        v = sb("v", [P, GENS, TT, P], F32)
        probs = sb("probs", [P, PROB_SLOTS, HALF], F32)
        ones = sb("ones", [P, D], F32)
        mx = sb("mx", [P, 2, HG, TT], F32)
        mxall = sb("mxall", [P, HG, TT], F32)
        m32 = sb("m32", [P, HG * TT], F32)
        mparts = sb("mparts", [P, P // (HG * TT), HG * TT], F16)
        mt = sb("mt", [2 * HG * TT, P], F16)
        o_raw = sb("o_raw", [P, HALF], F32)
        l_raw = sb("l_raw", [P, HALF], F32)
        l_inv = sb("l_inv", [P, HALF], F32)
        o_norm = sb("o_norm", [P, HALF], F32)
        o_part = sb("o_part", [P, 2, HL, HALF], F16)

        score_ps = ps("score_ps", [P, SCORE_BANKS, HALF])
        max_ps = ps("max_ps", [P, MAX_BANKS, HALF])
        proj_ps = ps("proj_ps", [P, HALF])
        out_ps = ps("out_ps", [P, HALF])
        sum_ps = ps("sum_ps", [P, HALF])

        setup = sem("setup")
        xt_loaded = [sem("xt_loaded0"), sem("xt_loaded1")]
        proj_ready, proj_read, hi_done = sem("proj_ready"), sem("proj_read"), sem("hi_done")
        stage_ready, stacked = sem("stage_ready"), sem("stacked")
        chunk_ready, chunk_read, max_stored = sem("chunk_ready"), sem("chunk_read"), sem("max_stored")
        max_step, max_ready = sem("max_step"), sem("max_ready")
        max_t_ready, max_t_copied, max_rows = sem("max_t_ready"), sem("max_t_copied"), sem("max_rows")
        scores_ready, exp_done, pv_done = sem("scores_ready"), sem("exp_done"), sem("pv_done")
        sums_ready, out_copied, l_copied = sem("sums_ready"), sem("out_copied"), sem("l_copied")
        norm_step, o_ready, o_stored = sem("norm_step"), sem("o_ready"), [sem("o_stored0"), sem("o_stored1")]
        block = ctx.enter_context(nc.Block())

        def groups(eng, body):
            body(0, 0, 0, lambda k: True)
            with eng.Fori(0, B - 1) as b:
                for g in range(1, NG):
                    body(b * NG + g, g, b, lambda k: True)
                body(b * NG + NG, 0, b + 1, lambda k: True)
            for g in range(1, NG):
                body((B - 1) * NG + g, g, B - 1, lambda k, g=g: g + k < NG)

        @block.sync
        def _(sp):
            def load_tokens(b, half):
                cols = slice(half * HALF, (half + 1) * HALF)
                sp.dma_start(xt[:, :, :, cols], xt_dram[bass.ds(b, 1), :, :, :, cols]
                             .rearrange("o p l e t -> p (o l) e t")).then_inc(xt_loaded[half], 16)

            def stack_group(gen, group):
                for which, dst, order in ((0, qs, (0, 1, 0)), (1, ks, (0, 0, 1))):
                    sp.wait_ge(proj_read, group * PROJ_TILES + 2 * which + 2 + 1)
                    for h in range(HG):
                        for r, l in enumerate(order):
                            sp.dma_start(dst[r * D:(r + 1) * D, gen, h, :], stage[h * D:(h + 1) * D, which, l, :]
                                         ).then_inc(stacked, 16)

            def max_rows_in(gen, group):
                sp.wait_ge(max_t_copied, group + 1)
                if not (isinstance(group, int) and group == 0):
                    sp.wait_ge(max_rows, group * 16)
                sp.dma_start(m_dram.rearrange("r h (i q) -> (r h i) q", q=P), mt[:, :]).then_inc(max_stored, 16)
                sp.wait_ge(max_stored, 16 * (group + 1))
                sp.dma_start(qs[3 * D:3 * D + 2, gen, :, :], m_dram).then_inc(max_rows, 16)

            def store_output(n, g, half):
                sp.wait_ge(o_ready, n * 2 + half + 1)
                sp.dma_start(o_dram[bass.ds(n, 1), :, :, half * HALF:(half + 1) * HALF]
                             .rearrange("o p l t -> p (o l) t"), o_part[:, half, :, :]).then_inc(o_stored[half], 16)

            for half in range(2):
                sp.sem_inc(o_stored[half], 16)
            load_tokens(0, 0)
            load_tokens(0, 1)
            stack_group(0, 0)
            stack_group(1, 1)
            max_rows_in(0, 0)

            def body(n, g, b, ahead):
                if not (isinstance(n, int) and n == 0):
                    store_output(n - 1, (g - 1) % NG, 1)
                if ahead(2):
                    stack_group((g + 2) % GENS, n + 2)
                if ahead(1):
                    max_rows_in((g + 1) % GENS, n + 1)
                if g == 1 and ahead(3):
                    for half in range(2):
                        sp.wait_ge(proj_ready, (n + 2) * PROJ_TILES + PROJ_TILES - 1 + half)
                        load_tokens(b + 1, half)
                store_output(n, g, 0)

            groups(sp, body)
            store_output(B * NG - 1, NG - 1, 1)
            for half in range(2):
                sp.wait_ge(o_stored[half], 16 * B * NG + 16)

        @block.gpsimd
        def _(pool):
            nc.gpsimd.memset(ks[3 * D:P, :, :, :], SHIFT_ROW).then_inc(setup, 1)
            pool.wait_ge(setup, 1)
            nc.gpsimd.memset(ones[:, :], 1.0).then_inc(setup, 1)
            nc.gpsimd.memset(mx[:, :, :, :], MASKED).then_inc(setup, 1)
            nc.gpsimd.memset(mparts[:, :, :], 0.0).then_inc(setup, 1)

        @block.tensor
        def _(pe):
            pe.sem_inc(pv_done, PROB_SLOTS)

            def projection(g, tile, step, group):
                if step == 0:
                    pe.wait_ge(proj_read, group * PROJ_TILES + tile + 1)
                e, k = divmod(step, len(PASSES))
                a, c = PASSES[k]
                start, stop = step == 0, step == PROJ_STEPS - 1
                if tile < 4:
                    which, half = divmod(tile, 2)
                    last = nc.tensor.matmul(proj_ps[:, :],
                                            w_qkv[:, a, e, which * E + g * P:which * E + (g + 1) * P],
                                            xt[:, c, e, half * HALF:(half + 1) * HALF], start=start, stop=stop)
                else:
                    for i in range(EC):
                        t = (tile - 4) * EC + i
                        last = nc.tensor.matmul(proj_ps[:, i * P:(i + 1) * P], xt[:, a, e, t * P:(t + 1) * P],
                                                w_qkv[:, c, e, 2 * E + g * P:2 * E + (g + 1) * P],
                                                start=start and i == 0, stop=stop, skip_group_check=True)
                if stop:
                    last.then_inc(proj_ready, 1)

            def max_chunk(gen, c, count, group):
                h, i, k0, width, diagonal = chunk_block(c)
                if c == 0 and not (isinstance(count, int) and count == 0):
                    pe.wait_ge(max_t_copied, group)
                pe.wait_ge(chunk_read, count + 1)
                bank = max_ps[:, c % MAX_BANKS]
                last = nc.tensor.matmul(bank[:, 0:width], qs[0:3 * D, gen, h, i * P:(i + 1) * P],
                                        ks[0:3 * D, gen, h, k0:k0 + width], start=True, stop=not diagonal)
                if diagonal:
                    last = nc.tensor.matmul(bank[:, width - P:width], identb[:, :], neg_m[:, :], start=False, stop=True)
                last.then_inc(chunk_ready, 1)

            def max_transpose(group):
                pe.wait_ge(max_ready, group + 1)
                nc.tensor.transpose(max_ps[:, 0].bitcast(F16)[:, 0:P], mparts[:, :, :].rearrange("p r c -> p (r c)"),
                                    ident16[:, :]).then_inc(max_t_ready, 1)

            def scores(gen, u, count):
                _, h, j, q0 = unit_block(u)
                half = unit_block(u)[0]
                diagonal = j * P >= half * HALF
                pe.wait_ge(exp_done, count + 1)
                bank = score_ps[:, u % SCORE_BANKS]
                last = nc.tensor.matmul(bank[:, 0:HALF - q0], ks[0:3 * D + 2, gen, h, j * P:(j + 1) * P],
                                        qs[0:3 * D + 2, gen, h, half * HALF + q0:(half + 1) * HALF],
                                        start=True, stop=not diagonal)
                if diagonal:
                    last = nc.tensor.matmul(bank[:, 0:P], identb[:, :], neg_s[:, :], start=False, stop=True)
                last.then_inc(scores_ready, 1)

            def values(gen, u, count, halves):
                half, h, j, q0 = unit_block(u)
                end = EC - 1 if half == 0 else TT - 1
                pe.wait_ge(exp_done, count + 1 + SCORE_BANKS)
                if h == 0 and j == 0:
                    pe.wait_ge(out_copied, halves + 1)
                    pe.wait_ge(l_copied, halves + 1)
                pt = probs[:, u % PROB_SLOTS, 0:HALF - q0]
                rows = slice(h * D, (h + 1) * D)
                nc.tensor.matmul(out_ps[rows, q0:HALF], v[:, gen, j, rows], pt, start=(j == 0), stop=(j == end),
                                 tile_position=(0, h * D))
                last = nc.tensor.matmul(sum_ps[rows, q0:HALF], ones[:, :], pt, start=(j == 0), stop=(j == end),
                                        tile_position=(0, h * D))
                last.then_inc(pv_done, 1)

            pe.wait_ge(setup, 4)
            for half in range(2):
                pe.wait_ge(xt_loaded[half], 16)
            for tile in range(PROJ_TILES):
                for step in range(PROJ_STEPS):
                    projection(0, tile, step, 0)
            for tile in range(PROJ_TILES):
                for step in range(PROJ_STEPS):
                    projection(1, tile, step, 1)
            pe.wait_ge(stacked, 16 * STACK_DMAS)
            for c in range(CHUNKS):
                max_chunk(0, c, c, 0)
            max_transpose(0)

            def body(n, g, b, ahead):
                first = isinstance(n, int) and n == 0
                for u in range(UNITS):
                    if u == 0:
                        pe.wait_ge(max_rows, n * 16 + 16)
                    scores(g, u, n * UNITS + u)
                    if ahead(1):
                        if u == 0:
                            pe.wait_ge(stacked, n * (16 * STACK_DMAS) + 32 * STACK_DMAS)
                        for c in CHUNKS_AT[u]:
                            max_chunk((g + 1) % GENS, c, (n + 1) * CHUNKS + c, n + 1)
                        if u == MAX_T_AT:
                            max_transpose(n + 1)
                    if ahead(2):
                        tile, steps = proj_steps_at(u)
                        for step in steps:
                            if g == 2 and step == 0 and tile < 2:
                                pe.wait_ge(xt_loaded[tile], b * 16 + 32)
                            projection((g + 2) % NG, tile, step, n + 2)
                    if u >= LAG:
                        past = u - LAG
                        values(g, past, n * UNITS + past, n * 2 + (0 if past < HG * EC else 1))
                    elif not first:
                        past = u - LAG + UNITS
                        values((g - 1) % GENS, past, n * UNITS - UNITS + past, n * 2 - 1)
            groups(pe, body)
            for past in range(UNITS - LAG, UNITS):
                values(NG - 1, past, (B * NG - 1) * UNITS + past, B * NG * 2 - 1)

        @block.scalar
        def _(act):
            act.sem_inc(exp_done, SCORE_BANKS)
            act.sem_inc(out_copied, 1)

            def copy_projection(gen, tile, group):
                act.wait_ge(proj_ready, group * PROJ_TILES + tile + 1)
                if tile < 4:
                    which, half = divmod(tile, 2)
                    if tile == 0 and not (isinstance(group, int) and group == 0):
                        act.wait_ge(stacked, group * (16 * STACK_DMAS))
                    nc.scalar.activation(stage[:, which, 0, half * HALF:(half + 1) * HALF], proj_ps[:, :],
                                         ACT.Copy).then_inc(hi_done, 1)
                else:
                    t0 = (tile - 4) * EC
                    nc.scalar.activation(v[:, gen, t0:t0 + EC, :], proj_ps[:, :].rearrange("p (t f) -> p t f", t=EC),
                                         ACT.Copy).then_inc(proj_read, 1)

            def copy_output(m, half):
                k = m * 2 + half
                act.wait_ge(pv_done, m * UNITS + (HG * EC if half == 0 else UNITS) + PROB_SLOTS)
                act.wait_ge(norm_step, k * NORM_STEPS + NORM_STEPS)
                nc.scalar.activation(o_raw[:, :], out_ps[:, :], ACT.Copy).then_inc(out_copied, 1)

            for group in range(2):
                for tile in range(PROJ_TILES):
                    copy_projection(group, tile, group)

            def body(n, g, b, ahead):
                for u in range(UNITS):
                    q0 = unit_block(u)[3]
                    count = n * UNITS + u
                    act.wait_ge(scores_ready, count + 1)
                    act.wait_ge(pv_done, count + 1)
                    nc.scalar.activation(probs[:, u % PROB_SLOTS, 0:HALF - q0],
                                         score_ps[:, u % SCORE_BANKS, 0:HALF - q0], ACT.Exp,
                                         scale=exp_scale[:, 0:1]).then_inc(exp_done, 1)
                    if u == COPY_AT[0]:
                        copy_output(n, 0)
                    if u == COPY_AT[1] and not (isinstance(n, int) and n == 0):
                        copy_output(n - 1, 1)
                    if ahead(2) and u >= 1 and proj_tile_done(u - 1) is not None:
                        tile = proj_tile_done(u - 1)
                        copy_projection((g + 2) % GENS, tile, n + 2)

            groups(act, body)
            copy_output(B * NG - 1, 1)

        @block.vector
        def _(dve):
            dve.sem_inc(proj_read, 1)
            dve.sem_inc(chunk_read, MAX_BANKS)
            dve.sem_inc(l_copied, 1)
            dve.sem_inc(norm_step, NORM_STEPS)
            dve.wait_ge(setup, 4)

            def low_parts(tile, group):
                which, half = divmod(tile, 2)
                cols = slice(half * HALF, (half + 1) * HALF)
                dve.wait_ge(hi_done, group * 4 + tile + 1)
                nc.vector.tensor_tensor(stage[:, which, 1, cols], proj_ps[:, :], stage[:, which, 0, cols],
                                        ALU.subtract).then_inc(proj_read, 1)

            def reduce_chunk(c, count):
                h, i, k0, width, _ = chunk_block(c)
                dve.wait_ge(chunk_ready, count + 1)
                nc.vector.tensor_reduce(mx[:, 1 if k0 else 0, h, i:i + 1], max_ps[:, c % MAX_BANKS, 0:width],
                                        AX_X, ALU.max).then_inc(chunk_read, 1)

            def prepare_max(group):
                dve.wait_ge(chunk_read, group * CHUNKS + CHUNKS + MAX_BANKS)
                nc.vector.tensor_tensor(mxall[:, :, :], mx[:, 0], mx[:, 1], ALU.max).then_inc(max_step, 1)
                dve.wait_ge(max_step, group * 3 + 1)
                nc.vector.tensor_scalar(m32[:, :], mxall[:, :, :].rearrange("p h i -> p (h i)"), -1.0 / SHIFT_ROW,
                                        None, ALU.mult).then_inc(max_step, 1)
                dve.wait_ge(max_step, group * 3 + 2)
                nc.vector.tensor_copy(mparts[:, 0], m32[:, :]).then_inc(max_step, 1)
                dve.wait_ge(max_step, group * 3 + 3)
                nc.vector.tensor_tensor(mparts[:, 1], m32[:, :], mparts[:, 0], ALU.subtract).then_inc(max_ready, 1)

            def copy_max_t(group):
                dve.wait_ge(max_t_ready, group + 1)
                if not (isinstance(group, int) and group == 0):
                    dve.wait_ge(max_rows, group * 16)
                nc.vector.tensor_copy(mt[:, :], max_ps[:, 0].bitcast(F16)[0:2 * HG * TT, 0:P]
                                      ).then_inc(max_t_copied, 1)

            def copy_sums(n, half):
                dve.wait_ge(pv_done, n * UNITS + (HG * EC if half == 0 else UNITS) + PROB_SLOTS)
                nc.vector.tensor_copy(l_raw[:, :], sum_ps[:, :]).then_inc(l_copied, 1)

            def invert(n, half, quarter):
                k = n * 2 + half
                cols = slice(quarter * P, (quarter + 1) * P)
                if quarter == 0:
                    dve.wait_ge(l_copied, k + 1 + 1)
                nc.vector.reciprocal(l_inv[:, cols], l_raw[:, cols]).then_inc(norm_step, 1)

            def normalise(n, half, step):
                k = n * 2 + half
                done = k * NORM_STEPS + NORM_STEPS
                dve.wait_ge(norm_step, done + 4 + step)
                if step == 0:
                    dve.wait_ge(out_copied, k + 1 + 1)
                    nc.vector.tensor_tensor(o_norm[:, :], o_raw[:, :], l_inv[:, :], ALU.mult).then_inc(norm_step, 1)
                elif step == 1:
                    dve.wait_ge(o_stored[half], n * 16 + 16)
                    nc.vector.tensor_copy(o_part[:, half, 0], o_norm[:, :]).then_inc(norm_step, 1)
                else:
                    nc.vector.tensor_tensor(o_part[:, half, 1], o_norm[:, :], o_part[:, half, 0], ALU.subtract
                                            ).then_inc(o_ready, 1)

            for group in range(2):
                for tile in range(4):
                    low_parts(tile, group)
            for c in range(CHUNKS):
                reduce_chunk(c, c)
            prepare_max(0)
            copy_max_t(0)

            def body(n, g, b, ahead):
                for u in range(UNITS):
                    if ahead(1):
                        for c in CHUNKS_AT[u]:
                            reduce_chunk(c, (n + 1) * CHUNKS + c)
                            if c == CHUNKS - 1:
                                prepare_max(n + 1)
                        if u == MAX_T_AT:
                            copy_max_t(n + 1)
                    if ahead(2) and u >= 1 and proj_tile_done(u - 1) in range(4):
                        tile = proj_tile_done(u - 1)
                        low_parts(tile, n + 2)
                    for half, m in ((0, n), (1, n - 1)):
                        if half == 1 and isinstance(n, int) and n == 0:
                            continue
                        if u == COPY_AT[half]:
                            copy_sums(m, half)
                        if u in INVERT_AT[half]:
                            invert(m, half, INVERT_AT[half].index(u))
                        if u in NORMALISE_AT[half]:
                            normalise(m, half, NORMALISE_AT[half].index(u))

            groups(dve, body)
            copy_sums(B * NG - 1, 1)
            for quarter in range(4):
                invert(B * NG - 1, 1, quarter)
            for step in range(3):
                normalise(B * NG - 1, 1, step)


GATES = 3
STEPS = 4


def recurrence(nc, xt_dram, w_gates, u_gates, inv, bias, c_start, c_scale, c_parts):
    with ExitStack() as ctx:
        def sb(name, shape, dt):
            return ctx.enter_context(nc.sbuf_tensor(f"rc_{name}", shape, dt))

        def sem(name):
            return ctx.enter_context(nc.semaphore(f"rc_{name}"))

        xt = sb("xt", [P, 2, HL, EC, HALF], F16)
        c = sb("c", [P, 2, EC, HALF], F32)
        act_out = sb("act_out", [P, 2, GATES, HALF], F32)
        fc = sb("fc", [P, HALF], F32)
        ig = sb("ig", [P, HALF], F32)
        total = sb("total", [P, HALF], F32)
        halfscale = sb("halfscale", [P, GATES, EC], F32)
        halfbias = sb("halfbias", [P, GATES, EC], F32)
        z = ctx.enter_context(nc.psum_tensor("rc_z", [P, 2 * GATES, HALF], F32))
        x_loaded, z_ready, z_read = [sem("x_loaded0"), sem("x_loaded1")], sem("z_ready"), sem("z_read")
        own, c_ready, consts = sem("own"), sem("c_ready"), sem("consts")
        block = ctx.enter_context(nc.Block())
        ROUND = EC * STEPS
        FACTOR = (0.5, 0.5, 1.0)

        @block.sync
        def _(sp):
            with sp.Fori(0, B // 2) as i:
                for s in range(STEPS):
                    t, half = divmod(s, 2)
                    sp.wait_ge(z_ready, i * (ROUND * GATES) + (s + 1) * EC * GATES)
                    sp.dma_start(xt[:, s % 2],
                                 xt_dram[bass.ds(i * 2 + t, 1), :, :, :, half * HALF:(half + 1) * HALF]
                                 .rearrange("o p l e t -> p (o l) e t")).then_inc(x_loaded[s % 2], 16)

        @block.tensor
        def _(pe):
            pe.sem_inc(z_ready, 2 * EC * GATES)
            with pe.Fori(0, B // 2) as i:
                for s in range(STEPS):
                    t, half = divmod(s, 2)
                    pe.wait_ge(x_loaded[s % 2], i * (8 * STEPS) + 16 * (s // 2 + 1))
                    for m in range(EC):
                        k = s * EC + m
                        for gate in range(GATES):
                            bank = z[:, (k % 2) * GATES + gate]
                            pe.wait_ge(z_read, i * (ROUND * GATES) + k * GATES + gate + 1)
                            for q, (a, l) in enumerate(PASSES):
                                for e in range(EC):
                                    nc.tensor.matmul(bank, w_gates[:, a, e, gate * E + m * P:gate * E + (m + 1) * P],
                                                     xt[:, s % 2, l, e, :], start=(q == 0 and e == 0), stop=False)
                            if m == 0 and gate == 0:
                                pe.wait_ge(c_ready, i * ROUND + s * EC + EC)
                            for q, (a, l) in enumerate(PASSES):
                                for e in range(EC):
                                    last = nc.tensor.matmul(
                                        bank, u_gates[:, a, e, gate * E + m * P:gate * E + (m + 1) * P],
                                        c_parts[:, half, t, l, e, :], start=False,
                                        stop=(q == len(PASSES) - 1 and e == EC - 1))
                            last.then_inc(z_ready, 1)

        @block.scalar
        def _(act):
            act.sem_inc(z_read, 2 * GATES)
            act.wait_ge(consts, GATES * 2)
            with act.Fori(0, B // 2) as i:
                for s in range(STEPS):
                    for m in range(EC):
                        k = s * EC + m
                        act.wait_ge(c_ready, i * ROUND + k + 7)
                        for gate in range(GATES):
                            act.wait_ge(z_ready, i * (ROUND * GATES) + k * GATES + gate + 1 + 2 * EC * GATES)
                            nc.scalar.activation(act_out[:, k % 2, gate], z[:, (k % 2) * GATES + gate], ACT.Tanh,
                                                 bias=halfbias[:, gate, m:m + 1],
                                                 scale=halfscale[:, gate, m:m + 1]).then_inc(z_read, 1)

        @block.vector
        def _(dve):
            for gate in range(GATES):
                nc.vector.tensor_scalar(halfscale[:, gate], inv[:, gate], FACTOR[gate], None, ALU.mult
                                        ).then_inc(consts, 1)
                nc.vector.tensor_scalar(halfbias[:, gate], bias[:, gate], FACTOR[gate], None, ALU.mult
                                        ).then_inc(consts, 1)
            ch = Chain(dve, own)
            for half in range(2):
                for m in range(EC):
                    ch.after(nc.vector.tensor_copy(c[:, half, m], c_start[:, m:m + 1].broadcast_to([P, HALF])))
                    ch.after(nc.vector.tensor_scalar(c_parts[:, half, 0, 0, m], c[:, half, m], c_scale[:, 0:1], None,
                                                     ALU.mult))
                    nc.vector.scalar_tensor_tensor(c_parts[:, half, 0, 1, m], c[:, half, m], c_scale[:, 0:1],
                                                   c_parts[:, half, 0, 0, m], ALU.mult, ALU.subtract
                                                   ).then_inc(c_ready, 1)
            before = ch.count
            LINKS = 5
            with dve.Fori(0, B // 2) as i:
                ch = Chain(dve, own, i * (ROUND * LINKS) + before)
                for s in range(STEPS):
                    t, half = divmod(s, 2)
                    for m in range(EC):
                        k = s * EC + m
                        dve.wait_ge(z_read, i * (ROUND * GATES) + (k + 1) * GATES + 2 * GATES)
                        f, g_in, g_cell = (act_out[:, k % 2, gate] for gate in range(GATES))
                        new = c_parts[:, half, 1 - t]
                        ch.after(nc.vector.scalar_tensor_tensor(fc[:, :], f, 1.0, c[:, half, m], ALU.add, ALU.mult))
                        ch.after(nc.vector.scalar_tensor_tensor(ig[:, :], g_in, 1.0, g_cell, ALU.add, ALU.mult))
                        ch.after(nc.vector.tensor_tensor(total[:, :], fc[:, :], ig[:, :], ALU.add))
                        ch.after(nc.vector.tensor_scalar(c[:, half, m], total[:, :], 0.5, None, ALU.mult))
                        ch.after(nc.vector.tensor_scalar(new[:, 0, m], c[:, half, m], c_scale[:, 0:1], None, ALU.mult))
                        nc.vector.scalar_tensor_tensor(new[:, 1, m], c[:, half, m], c_scale[:, 0:1], new[:, 0, m],
                                                       ALU.mult, ALU.subtract).then_inc(c_ready, 1)


def output_layer(nc, xt_dram, x1, out, w_o, u_o, inv_dram, bo, c_parts):
    with ExitStack() as ctx:
        def sb(name, shape, dt):
            return ctx.enter_context(nc.sbuf_tensor(f"ol_{name}", shape, dt))

        def sem(name):
            return ctx.enter_context(nc.semaphore(f"ol_{name}"))

        def slots(name):
            return [sem(f"{name}{s}") for s in range(2)]

        xt = sb("xt", [P, 2, HL, EC, T], F16)
        res = sb("res", [P, 2, TT, E], F32)
        state = sb("state", [P, TT, E], F32)
        scaled = sb("scaled", [P, 2, E], F32)
        summed = sb("summed", [P, 2, E], F32)
        h = sb("h", [P, 2, E], F32)
        inv_row = sb("inv_row", [P, E], F32)
        bo_row = sb("bo_row", [P, E], F32)
        z = ctx.enter_context(nc.psum_tensor("ol_z", [P, 4, E], F32))
        rows, x_loaded, res_loaded = sem("rows"), slots("x_loaded"), slots("res_loaded")
        z_ready, z_read, summed_ready, h_ready = sem("z_ready"), sem("z_read"), sem("summed_ready"), sem("h_ready")
        done, stored = sem("done"), slots("stored")
        block = ctx.enter_context(nc.Block())
        BANKS = 4

        @block.sync
        def _(sp):
            sp.dma_start(inv_row[:, :], inv_dram.partition_broadcast(P)).then_inc(rows, 16)
            sp.dma_start(bo_row[:, :], bo.partition_broadcast(P)).then_inc(rows, 16)
            def load(b, s):
                sp.dma_start(xt[:, s], xt_dram[bass.ds(b, 1)].rearrange("o p l e t -> p (o l) e t")
                             ).then_inc(x_loaded[s], 16)
                sp.dma_start(res[:, s], x1[bass.ds(b, 1)].rearrange("o (t p) e -> p (o t) e", p=P)
                             ).then_inc(res_loaded[s], 16)

            def pair(i, last):
                for s in range(2):
                    if not (last and s == 1):
                        sp.wait_ge(stored[1 - s], i * 16 + (16 if s == 0 else 32))
                        load(i * 2 + s + 1, 1 - s)
                    sp.wait_ge(done, i * (2 * TT) + (s + 1) * TT)
                    sp.dma_start(out[bass.ds(i * 2 + s, 1)].rearrange("o (t p) e -> p (o t) e", p=P), res[:, s]
                                 ).then_inc(stored[s], 16)

            for s in range(2):
                sp.sem_inc(stored[s], 16)
            load(0, 0)
            with sp.Fori(0, B // 2 - 1) as i:
                pair(i, False)
            pair(B // 2 - 1, True)
            for s in range(2):
                sp.wait_ge(stored[s], 16 * (B // 2) + 16)

        @block.tensor
        def _(pe):
            for n in range(TT):
                half, col = divmod(n, EC)
                if n >= BANKS:
                    pe.wait_ge(z_read, n - BANKS + 1)
                for q, (a, l) in enumerate(PASSES):
                    for e in range(EC):
                        last = nc.tensor.matmul(z[:, n % BANKS], c_parts[:, half, 0, a, e, col * P:(col + 1) * P],
                                                u_o[:, l, e, :], start=(q == 0 and e == 0),
                                                stop=(q == len(PASSES) - 1 and e == EC - 1))
                last.then_inc(z_ready, 1)
            with pe.Fori(0, B // 2) as i:
                for s in range(2):
                    pe.wait_ge(x_loaded[s], i * 16 + 16)
                    for t in range(TT):
                        n = i * (2 * TT) + s * TT + t + TT
                        pe.wait_ge(z_read, n - BANKS + 1)
                        for q, (a, l) in enumerate(PASSES):
                            for e in range(EC):
                                last = nc.tensor.matmul(z[:, t % BANKS], xt[:, s, a, e, t * P:(t + 1) * P],
                                                        w_o[:, l, e, :], start=(q == 0 and e == 0),
                                                        stop=(q == len(PASSES) - 1 and e == EC - 1))
                        last.then_inc(z_ready, 1)

        @block.scalar
        def _(act):
            with act.Fori(0, B // 2) as i:
                for s in range(2):
                    for t in range(TT):
                        n = i * (2 * TT) + s * TT + t
                        act.wait_ge(summed_ready, n + TT + 1)
                        nc.scalar.activation(h[:, t % 2], summed[:, t % 2], ACT.Tanh).then_inc(h_ready, 1)

        @block.vector
        def _(dve):
            dve.wait_ge(rows, 32)
            for n in range(TT):
                dve.wait_ge(z_ready, n + 1)
                nc.vector.tensor_tensor(scaled[:, n % 2], z[:, n % BANKS], inv_row[:, :], ALU.mult).then_inc(z_read, 1)
                dve.wait_ge(z_read, n + 1)
                nc.vector.tensor_tensor(state[:, n], scaled[:, n % 2], bo_row[:, :], ALU.add).then_inc(summed_ready, 1)
            dve.wait_ge(summed_ready, TT)
            with dve.Fori(0, B // 2) as i:
                for s in range(2):
                    dve.wait_ge(res_loaded[s], i * 16 + 16)

                    def residual(i, s, t):
                        n = i * (2 * TT) + s * TT + t
                        dve.wait_ge(h_ready, n + 1)
                        nc.vector.tensor_tensor(res[:, s, t], res[:, s, t], h[:, t % 2], ALU.add).then_inc(done, 1)

                    for t in range(TT):
                        n = i * (2 * TT) + s * TT + t + TT
                        dve.wait_ge(z_ready, n + 1)
                        nc.vector.tensor_tensor(scaled[:, t % 2], z[:, t % BANKS], inv_row[:, :], ALU.mult
                                                ).then_inc(z_read, 1)
                        dve.wait_ge(z_read, n + 1)
                        if t >= 2:
                            residual(i, s, t - 2)
                        nc.vector.tensor_tensor(summed[:, t % 2], scaled[:, t % 2], state[:, t], ALU.add
                                                ).then_inc(summed_ready, 1)
                    residual(i, s, TT - 2)
                    residual(i, s, TT - 1)


def build(nc, x, w_in, w_out, wf, uf, bf, wi, ui, bi, wc, uc, bc, wo, uo, bo, in_c, out):
    def scratch(name, shape, dt):
        return nc.dram_tensor(name, shape, dt, kind="Internal").ap()

    xt1 = scratch("xt1", (B, P, HL, EC, T), F16)
    xt2 = scratch("xt2", (B, P, HL, EC, T), F16)
    ot = scratch("ot", (B * NG, P, HL, T), F16)
    x1 = scratch("x1", (B, T, E), F32)
    m_dram = scratch("m_dram", (2, HG, T), F16)
    v_row = scratch("v_row", (E,), F32)
    out_row = scratch("out_row", (E,), F32)
    o_row = scratch("o_row", (E,), F32)
    with ExitStack() as ctx:
        ctx.enter_context(nc.allow_non_contiguous_dma(reason="a few vectors of 512 numbers, spread over the partitions"))

        def sb(name, shape, dt, c=ctx):
            return c.enter_context(nc.sbuf_tensor(name, shape, dt))

        ident16 = sb("ident16", [P, P], F16)
        identb = sb("identb", [P, P], BF16)
        neg_m = sb("neg_m", [P, P], BF16)
        neg_s = sb("neg_s", [P, P], BF16)
        bias = sb("bias", [P, GATES, EC], F32)
        c_start = sb("c_start", [P, EC], F32)
        c_row = sb("c_row", [P, E], F32)
        c_top = sb("c_top", [P, 1], F32)
        c_inv = sb("c_inv", [P, 1], F32)
        c_scale = sb("c_scale", [P, 1], F32)
        exp_scale = sb("exp_scale", [P, 1], F32)

        with nc.semaphore("made") as made, nc.semaphore("consts_in") as consts_in, nc.semaphore("c_steps") as c_steps, \
                nc.Block() as block:
            @block.sync
            def _(sp):
                for g, v in enumerate((bf, bi, bc)):
                    sp.dma_start(bias[:, g, :], v.rearrange("(t p) -> p t", p=P)).then_inc(consts_in, 16)
                sp.dma_start(c_start[:, :], in_c.rearrange("(t p) -> p t", p=P)).then_inc(consts_in, 16)
                sp.dma_start(c_row[:, :], in_c.partition_broadcast(P)).then_inc(consts_in, 16)

            @block.gpsimd
            def _(pool):
                for tile, value in ((ident16, 0.0), (identb, 0.0), (neg_m, 0.0), (neg_s, 0.0)):
                    nc.gpsimd.memset(tile[:, :], value).then_inc(made, 1)
                pool.wait_ge(made, 4)
                for tile in (ident16, identb):
                    nc.gpsimd.affine_select(out=tile[:, :], in_=tile[:, :], compare_op=ALU.not_equal, fill=1.0, base=0,
                                            pattern=[[-1, P]], channel_multiplier=1)
                nc.gpsimd.affine_select(out=neg_m[:, :], in_=neg_m[:, :], compare_op=ALU.is_ge, fill=MASKED, base=0,
                                        pattern=[[-1, P]], channel_multiplier=1)
                nc.gpsimd.affine_select(out=neg_s[:, :], in_=neg_s[:, :], compare_op=ALU.is_ge, fill=MASKED, base=0,
                                        pattern=[[1, P]], channel_multiplier=-1).then_inc(made, 1)
                pool.wait_ge(made, 5)

            @block.vector
            def _(dve):
                ch = Chain(dve, c_steps)
                dve.wait_ge(consts_in, 80)
                ch.after(nc.vector.tensor_reduce(c_top[:, :], c_row[:, :], AX_X, ALU.max, apply_absolute_value=True))
                ch.after(nc.vector.tensor_scalar(c_inv[:, :], c_top[:, :], 1.0, None, ALU.max))
                ch.after(nc.vector.tensor_scalar(c_inv[:, :].bitcast(U32), c_inv[:, :].bitcast(U32), EXPONENT, None,
                                                 ALU.bitwise_and))
                ch.after(nc.vector.reciprocal(c_scale[:, :], c_inv[:, :]))

        with ExitStack() as first:
            w_qkv = sb("w_qkv", [P, HL, EC, 3 * E], F16, first)
            w_o1 = sb("w_o1", [P, HL, EC, E], F16, first)
            inv1 = sb("inv1", [P, 4, EC], F32, first)
            prepare_weights(nc, "pa", [[(w_in[2 * E:3 * E], w_qkv, 2 * E)], [(w_in[0:E], w_qkv, 0)],
                                       [(w_in[E:2 * E], w_qkv, E)], [(w_out, w_o1, 0)]],
                            inv1, ident16, (1, 2), scratch_v=(0, v_row))
            with nc.semaphore("row_out") as row_out, nc.semaphore("scale_set") as scale_set, nc.Block() as block:
                @block.sync
                def _(sp):
                    sp.dma_start(out_row.rearrange("(t p) -> p t", p=P), inv1[:, 3, :]).then_inc(row_out, 16)
                    sp.wait_ge(row_out, 16)

                @block.vector
                def _(dve):
                    nc.vector.scalar_tensor_tensor(exp_scale[:, :], inv1[:, 1, 0:1], D ** -0.5, inv1[:, 2, 0:1],
                                                   ALU.mult, ALU.mult).then_inc(scale_set, 1)
                    dve.wait_ge(scale_set, 1)
            normalise_tokens(nc, "n1", x, xt1, ident16)
            attention(nc, xt1, ot, m_dram, w_qkv, exp_scale, ident16, identb, neg_m, neg_s)
            normalise_tokens(nc, "n2", x, xt2, ident16, outproj=(ot, w_o1, out_row, x1))

        w_gates = sb("w_gates", [P, HL, EC, GATES * E], F16)
        u_gates = sb("u_gates", [P, HL, EC, GATES * E], F16)
        w_o = sb("w_o", [P, HL, EC, E], F16)
        u_o = sb("u_o", [P, HL, EC, E], F16)
        inv2 = sb("inv2", [P, 4, EC], F32)
        c_parts = sb("c_parts", [P, 2, 2, HL, EC, HALF], F16)
        prepare_weights(nc, "pb", [[(w, w_gates, g * E), (u, u_gates, g * E)]
                                   for g, (w, u) in enumerate(((wf, uf), (wi, ui), (wc, uc)))] +
                        [[(wo, w_o, 0), (uo, u_o, 0)]], inv2, ident16, (), c_scale=c_inv)
        with nc.semaphore("row_out2") as row_out2, nc.Block() as block:
            @block.sync
            def _(sp):
                sp.dma_start(o_row.rearrange("(t p) -> p t", p=P), inv2[:, 3, :]).then_inc(row_out2, 16)
                sp.wait_ge(row_out2, 16)
        recurrence(nc, xt2, w_gates, u_gates, inv2, bias, c_start, c_scale, c_parts)
        output_layer(nc, xt2, x1, out, w_o, u_o, o_row, bo, c_parts)


INS = ("L0_attn_query", "L0_attn_in_proj_weight", "L0_attn_out_proj_weight", "L0_ffn_wf", "L0_ffn_uf", "L0_ffn_bf",
       "L0_ffn_wi", "L0_ffn_ui", "L0_ffn_bi", "L0_ffn_wc", "L0_ffn_uc", "L0_ffn_bc", "L0_ffn_wo", "L0_ffn_uo",
       "L0_ffn_bo", "L0_ffn_in_c")


def kernel(**inputs):
    import numpy as _np
    import concourse.bacc as _bacc
    from concourse import mybir as _mybir
    from concourse.bass_utils import run_bass_kernel_spmd as _run

    nc = _bacc.Bacc("TRN2", target_bir_lowering=False, num_devices=1)
    arrays, args = {}, []
    for name in INS:
        a = _np.ascontiguousarray(inputs[name])
        arrays[f"in_{name}"] = a
        args.append(nc.dram_tensor(f"in_{name}", a.shape, _mybir.dt.from_np(a.dtype), kind="ExternalInput").ap())
    args.append(nc.dram_tensor("out_0", (B, T, E), F32, kind="ExternalOutput").ap())
    nc.disable_value_cache = True
    build(nc, *args)
    r = _run(nc, [arrays], core_ids=[0])
    return r.results[0]["out_0"]
```
